# Optimizing a Trainium2 kernel written in Bass

```python
import numpy as np
import jax
import jax.numpy as jnp

def _softmax(x, axis=-1):
    return jax.nn.softmax(x, axis=axis)

def _gelu(x):
    return jax.nn.gelu(x, approximate=True)

def _silu(x):
    return jax.nn.silu(x)

def _sigmoid(x):
    return jax.nn.sigmoid(x)

def _layernorm(x, axis=-1, eps=1e-05):
    m = jnp.mean(x, axis=axis, keepdims=True)
    v = jnp.var(x, axis=axis, keepdims=True)
    return (x - m) / jnp.sqrt(v + eps)

def _scatter_add(tgt, idx, src, axis=0):
    return tgt.at[idx].add(src)

def _segment_sum(src, seg, n):
    return jax.ops.segment_sum(src, seg, n)
kernel_name = 'mk_adaln_d2_jaxref_r8_339e1a'

def setup_inputs(seed: int=0):
    np.random.seed(seed)
    _w = jnp.asarray

    def _L0_attn_setup():
        import jax, jax.numpy as jnp
        import numpy as np
        B_, L_, DM, DIN, N_, K_, R_ = (1, 128, 128, 256, 16, 4, 64)
        key = jax.random.key(seed)
        ks = jax.random.split(key, 10)
        rn = lambda k, shape, s: jax.random.normal(k, shape, jnp.float32) * s
        dt_min, dt_max = (0.001, 0.1)
        u = jax.random.uniform(ks[6], (DIN,), jnp.float32)
        dt = jnp.exp(u * (np.log(dt_max) - np.log(dt_min)) + np.log(dt_min))
        b_dt = dt + jnp.log(-jnp.expm1(-dt))
        A_log = jnp.log(jnp.broadcast_to(jnp.arange(1, N_ + 1, dtype=jnp.float32), (DIN, N_)))
        return {'x': rn(ks[0], (B_, L_, DM), 1.0), 'W_in': rn(ks[1], (2 * DIN, DM), 0.02), 'conv_w': rn(ks[2], (DIN, K_), 0.1), 'conv_b': rn(ks[3], (DIN,), 0.02), 'W_x': rn(ks[4], (R_ + 2 * N_, DIN), 0.02), 'W_dt': rn(ks[5], (DIN, R_), R_ ** (-0.5)), 'b_dt': b_dt, 'A_log': A_log, 'D_param': jnp.ones((DIN,), jnp.float32), 'W_out': rn(ks[7], (DM, DIN), 0.02)}
    _L0_attn_in = _L0_attn_setup()

    def _L0_ffn_setup():
        import jax, jax.numpy as jnp
        import numpy as np
        B, N, C, F, E, K = (2, 256, 128, 512, 8, 2)
        key = jax.random.key(seed)
        k = jax.random.split(key, 6)
        xavier1 = float(np.sqrt(6.0 / (C + F)))
        xavier2 = float(np.sqrt(6.0 / (F + C)))
        return {'x': jax.random.normal(k[0], (B, N, C), dtype=jnp.float32), 'router_w': jax.random.normal(k[1], (E, C), dtype=jnp.float32) * 0.01, 'w1': jax.random.uniform(k[2], (E, F, C), dtype=jnp.float32, minval=-xavier1, maxval=xavier1), 'b1': jnp.zeros((E, F), dtype=jnp.float32), 'w2': jax.random.uniform(k[3], (E, C, F), dtype=jnp.float32, minval=-xavier2, maxval=xavier2), 'b2': jnp.zeros((E, C), dtype=jnp.float32)}
    _L0_ffn_in = _L0_ffn_setup()
    _L0_c = _w((lambda *s: np.random.randn(*s).astype(np.float32) * 0.05)(2, 128))
    _L0_wmod = _w((lambda *s: np.random.randn(*s).astype(np.float32) * 0.05)(128, 6 * 128) * 128 ** (-0.5))

    def _L1_attn_setup():
        import jax, jax.numpy as jnp
        import numpy as np
        B, L, D, N = (4, 512, 128, 128)
        EPS = 1e-05

        def _gated_scan(A, b):

            def combine(c1, c2):
                a1, u1 = c1
                a2, u2 = c2
                return (a1 * a2, a2 * u1 + u2)
            _, h = jax.lax.associative_scan(combine, (A, b), axis=1)
            return h
        key = jax.random.key(seed)
        ks = jax.random.split(key, 8)
        s = 0.02
        return {'x': jax.random.normal(ks[0], (B, L, D), jnp.float32), 'rms_weight': jnp.ones((D,), jnp.float32), 'w_A': jax.random.normal(ks[1], (D, N), jnp.float32) * s, 'b_A': jnp.zeros((N,), jnp.float32), 'w_x': jax.random.normal(ks[2], (D, N), jnp.float32) * s, 'w_sidegate': jax.random.normal(ks[3], (D, N), jnp.float32) * s, 'w_output': jax.random.normal(ks[4], (D, N), jnp.float32) * s, 'w_o': jax.random.normal(ks[5], (N, D), jnp.float32) * s}
    _L1_attn_in = _L1_attn_setup()

    def _L1_ffn_setup():
        import jax, jax.numpy as jnp
        import numpy as np
        TOPK = 2
        EPS = 1e-06
        key = jax.random.key(seed)
        ks = jax.random.split(key, 8)
        b, t, d, h, n = (2, 128, 128, 256, 16)
        x = jax.random.normal(ks[0], (b, t, d), dtype=jnp.float32)
        router_w = jax.random.normal(ks[1], (n, d), dtype=jnp.float32) * (1.0 / np.sqrt(d))
        router_bias = jnp.zeros((n,), dtype=jnp.float32)
        bank_mag = jax.random.normal(ks[2], (n, d, h), dtype=jnp.float32) * (1.0 / np.sqrt(d))
        bank_freq = jax.random.uniform(ks[3], (n, d, h), dtype=jnp.float32, minval=0.5, maxval=2.0) * (1.0 / np.sqrt(d))
        bank_phase = jax.random.uniform(ks[4], (n, h), dtype=jnp.float32, minval=-0.3, maxval=0.3)
        bank_down = jax.random.normal(ks[5], (n, h, d), dtype=jnp.float32) * (1.0 / np.sqrt(h))
        norm_w = jnp.ones((d,), dtype=jnp.float32)
        return {'x': x, 'router_w': router_w, 'router_bias': router_bias, 'bank_mag': bank_mag, 'bank_freq': bank_freq, 'bank_phase': bank_phase, 'bank_down': bank_down, 'norm_w': norm_w}
    _L1_ffn_in = _L1_ffn_setup()
    _L1_c = _w((lambda *s: np.random.randn(*s).astype(np.float32) * 0.05)(2, 128))
    _L1_wmod = _w((lambda *s: np.random.randn(*s).astype(np.float32) * 0.05)(128, 6 * 128) * 128 ** (-0.5))
    _d = {'L0_attn_x': _L0_attn_in['x'], 'L0_attn_W_in': _L0_attn_in['W_in'], 'L0_attn_conv_w': _L0_attn_in['conv_w'], 'L0_attn_conv_b': _L0_attn_in['conv_b'], 'L0_attn_W_x': _L0_attn_in['W_x'], 'L0_attn_W_dt': _L0_attn_in['W_dt'], 'L0_attn_b_dt': _L0_attn_in['b_dt'], 'L0_attn_A_log': _L0_attn_in['A_log'], 'L0_attn_D_param': _L0_attn_in['D_param'], 'L0_attn_W_out': _L0_attn_in['W_out'], 'L0_ffn_router_w': _L0_ffn_in['router_w'], 'L0_ffn_w1': _L0_ffn_in['w1'], 'L0_ffn_b1': _L0_ffn_in['b1'], 'L0_ffn_w2': _L0_ffn_in['w2'], 'L0_ffn_b2': _L0_ffn_in['b2'], 'L0_c': _L0_c, 'L0_wmod': _L0_wmod, 'L1_attn_rms_weight': _L1_attn_in['rms_weight'], 'L1_attn_w_A': _L1_attn_in['w_A'], 'L1_attn_b_A': _L1_attn_in['b_A'], 'L1_attn_w_x': _L1_attn_in['w_x'], 'L1_attn_w_sidegate': _L1_attn_in['w_sidegate'], 'L1_attn_w_output': _L1_attn_in['w_output'], 'L1_attn_w_o': _L1_attn_in['w_o'], 'L1_ffn_router_w': _L1_ffn_in['router_w'], 'L1_ffn_router_bias': _L1_ffn_in['router_bias'], 'L1_ffn_bank_mag': _L1_ffn_in['bank_mag'], 'L1_ffn_bank_freq': _L1_ffn_in['bank_freq'], 'L1_ffn_bank_phase': _L1_ffn_in['bank_phase'], 'L1_ffn_bank_down': _L1_ffn_in['bank_down'], 'L1_ffn_norm_w': _L1_ffn_in['norm_w'], 'L1_c': _L1_c, 'L1_wmod': _L1_wmod}
    _x0 = _d['L0_attn_x']
    _d['L0_attn_x'] = jax.random.normal(jax.random.fold_in(jax.random.key(seed), 1), (2, 1024, 128), dtype=_x0.dtype)
    del _x0
    return _d

def reference(L0_attn_x, L0_attn_W_in, L0_attn_conv_w, L0_attn_conv_b, L0_attn_W_x, L0_attn_W_dt, L0_attn_b_dt, L0_attn_A_log, L0_attn_D_param, L0_attn_W_out, L0_ffn_router_w, L0_ffn_w1, L0_ffn_b1, L0_ffn_w2, L0_ffn_b2, L0_c, L0_wmod, L1_attn_rms_weight, L1_attn_w_A, L1_attn_b_A, L1_attn_w_x, L1_attn_w_sidegate, L1_attn_w_output, L1_attn_w_o, L1_ffn_router_w, L1_ffn_router_bias, L1_ffn_bank_mag, L1_ffn_bank_freq, L1_ffn_bank_phase, L1_ffn_bank_down, L1_ffn_norm_w, L1_c, L1_wmod):

    def _L0_attn_ref(x, W_in, conv_w, conv_b, W_x, W_dt, b_dt, A_log, D_param, W_out):
        import jax, jax.numpy as jnp
        import numpy as np
        B_, L_, DM, DIN, N_, K_, R_ = (1, 128, 128, 256, 16, 4, 64)
        Din, K = conv_w.shape
        R = W_dt.shape[1]
        N = A_log.shape[1]
        xz = jnp.einsum('bld,ed->ble', x, W_in)
        xs, z = jnp.split(xz, 2, axis=-1)
        xt = jnp.transpose(xs, (0, 2, 1))
        xc = jax.lax.conv_general_dilated(xt, conv_w[:, None, :], (1,), [(K - 1, 0)], feature_group_count=Din)
        xc = jnp.transpose(xc, (0, 2, 1)) + conv_b
        xc = jax.nn.silu(xc)
        x_dbl = jnp.einsum('bld,ed->ble', xc, W_x)
        dt, Bm, Cm = jnp.split(x_dbl, [R, R + N], axis=-1)
        dt = jax.nn.softplus(jnp.einsum('blr,dr->bld', dt, W_dt) + b_dt)
        A = -jnp.exp(A_log)
        A_bar = jnp.exp(dt[..., None] * A)
        Bu = dt[..., None] * Bm[:, :, None, :] * xc[..., None]

        def comb(e1, e2):
            a1, b1 = e1
            a2, b2 = e2
            return (a2 * a1, a2 * b1 + b2)
        _, h_all = jax.lax.associative_scan(comb, (A_bar, Bu), axis=1)
        y = jnp.einsum('bldn,bln->bld', h_all, Cm) + D_param * xc
        y = y * jax.nn.silu(z)
        return jnp.einsum('bld,ed->ble', y, W_out)

    def _L0_ffn_ref(x, router_w, w1, b1, w2, b2):
        import jax, jax.numpy as jnp
        import numpy as np
        B, N, C, F, E, K = (2, 256, 128, 512, 8, 2)
        Bb, Nn, Cc = x.shape
        x_flat = x.reshape(-1, Cc)
        logits = jnp.einsum('tc,ec->te', x_flat, router_w)
        probs = jax.nn.softmax(logits, axis=-1)
        top_w, top_idx = jax.lax.top_k(probs, K)
        top_w = top_w / (jnp.sum(top_w, axis=-1, keepdims=True) + 1e-09)
        h = jnp.einsum('tc,efc->tef', x_flat, w1) + b1[None]
        h = jax.nn.relu(h)
        y = jnp.einsum('tef,ecf->tec', h, w2) + b2[None]
        sel = jnp.take_along_axis(y, top_idx[:, :, None], axis=1)
        out = jnp.einsum('tkc,tk->tc', sel, top_w)
        return out.reshape(Bb, Nn, Cc)

    def _L1_attn_ref(x, rms_weight, w_A, b_A, w_x, w_sidegate, w_output, w_o):
        import jax, jax.numpy as jnp
        import numpy as np
        B, L, D, N = (4, 512, 128, 128)
        EPS = 1e-05

        def _gated_scan(A, b):

            def combine(c1, c2):
                a1, u1 = c1
                a2, u2 = c2
                return (a1 * a2, a2 * u1 + u2)
            _, h = jax.lax.associative_scan(combine, (A, b), axis=1)
            return h
        residual = x
        norm = jnp.sqrt(jnp.mean(x * x, axis=-1, keepdims=True) + EPS)
        xn = x * (rms_weight / norm)
        A = jax.nn.sigmoid(jnp.einsum('bld,dn->bln', xn, w_A) + b_A)
        x_el = jnp.einsum('bld,dn->bln', xn, w_x)
        sidegate = jax.nn.sigmoid(jnp.einsum('bld,dn->bln', xn, w_output))
        gate = jax.nn.sigmoid(jnp.einsum('bld,dn->bln', xn, w_sidegate))
        h = _gated_scan(A, x_el * sidegate)
        y = gate * h
        return jnp.einsum('bln,nd->bld', y, w_o) + residual

    def _L1_ffn_ref(x, router_w, router_bias, bank_mag, bank_freq, bank_phase, bank_down, norm_w):
        import jax, jax.numpy as jnp
        import numpy as np
        TOPK = 2
        EPS = 1e-06
        b, t, d = x.shape
        scores = jnp.einsum('btd,nd->btn', x, router_w) + router_bias
        topv, topi = jax.lax.top_k(scores, TOPK)
        weights = jax.nn.softmax(topv, axis=-1)
        fx = x.reshape(b * t, d)
        mag = jnp.einsum('td,ndh->tnh', fx, bank_mag)
        freq = jnp.einsum('td,ndh->tnh', fx, bank_freq)
        hidden = jnp.tanh(mag) * jnp.cos(jax.nn.softplus(freq) + 0.1 + bank_phase[None, :, :])
        out_all = jnp.einsum('tnh,nhd->tnd', hidden, bank_down)
        ti = topi.reshape(b * t, TOPK)
        sel = jnp.take_along_axis(out_all, ti[:, :, None], axis=1)
        out = jnp.einsum('tkd,tk->td', sel, weights.reshape(b * t, TOPK)).reshape(b, t, d)
        out = out * jax.lax.rsqrt(jnp.mean(out * out, axis=-1, keepdims=True) + EPS) * norm_w
        return out
    x = L0_attn_x
    mod = (_silu(L0_c) @ L0_wmod).reshape(L0_c.shape[0], 6, 1, -1)
    sa, ca, ga, sb, cb, gb = (mod[:, 0], mod[:, 1], mod[:, 2], mod[:, 3], mod[:, 4], mod[:, 5])
    ga = (2 * (ga >= 0) - 1) * jnp.maximum(jnp.abs(ga), 0.25)
    gb = (2 * (gb >= 0) - 1) * jnp.maximum(jnp.abs(gb), 0.25)
    h = _layernorm(x, axis=-1) * (1 + ca) + sa
    x = x + ga * _L0_attn_ref(h, L0_attn_W_in, L0_attn_conv_w, L0_attn_conv_b, L0_attn_W_x, L0_attn_W_dt, L0_attn_b_dt, L0_attn_A_log, L0_attn_D_param, L0_attn_W_out)
    h = _layernorm(x, axis=-1) * (1 + cb) + sb
    x = x + gb * _L0_ffn_ref(h, L0_ffn_router_w, L0_ffn_w1, L0_ffn_b1, L0_ffn_w2, L0_ffn_b2)
    mod = (_silu(L1_c) @ L1_wmod).reshape(L1_c.shape[0], 6, 1, -1)
    sa, ca, ga, sb, cb, gb = (mod[:, 0], mod[:, 1], mod[:, 2], mod[:, 3], mod[:, 4], mod[:, 5])
    ga = (2 * (ga >= 0) - 1) * jnp.maximum(jnp.abs(ga), 0.25)
    gb = (2 * (gb >= 0) - 1) * jnp.maximum(jnp.abs(gb), 0.25)
    h = _layernorm(x, axis=-1) * (1 + ca) + sa
    x = x + ga * _L1_attn_ref(h, L1_attn_rms_weight, L1_attn_w_A, L1_attn_b_A, L1_attn_w_x, L1_attn_w_sidegate, L1_attn_w_output, L1_attn_w_o)
    h = _layernorm(x, axis=-1) * (1 + cb) + sb
    x = x + gb * _L1_ffn_ref(h, L1_ffn_router_w, L1_ffn_router_bias, L1_ffn_bank_mag, L1_ffn_bank_freq, L1_ffn_bank_phase, L1_ffn_bank_down, L1_ffn_norm_w)
    return x

_drawn_inputs = setup_inputs


def setup_inputs(seed=0):
    import zlib

    import numpy as np

    out = dict(_drawn_inputs(seed))
    spreads = {'L0_attn_D_param': (1.0, 0.2),
     'L0_ffn_b1': (0.0, 0.1),
     'L0_ffn_b2': (0.0, 0.1),
     'L1_attn_rms_weight': (1.0, 0.2),
     'L1_attn_b_A': (0.0, 0.1),
     'L1_ffn_router_bias': (0.0, 0.1),
     'L1_ffn_norm_w': (1.0, 0.2)}
    factors = {}
    for name, (base, spread) in spreads.items():
        noise = np.random.default_rng([zlib.crc32(name.encode()), seed]).standard_normal(out[name].shape)
        drawn = base * np.exp(spread * noise) if base else spread * noise
        out[name] = jnp.asarray(drawn.astype(out[name].dtype))
    for name, factor in factors.items():
        out[name] = (out[name] * factor).astype(out[name].dtype)
    return out
```

```python
from contextlib import ExitStack

import concourse.bass as bass
from concourse import mybir

F32 = mybir.dt.float32
BF16 = mybir.dt.bfloat16
I32 = mybir.dt.int32
ALU = mybir.AluOpType
ACT = mybir.ActivationFunctionType
AX = mybir.AxisListType.X

P = 128
BATCH = 2
T = 2048
NTILE = T // P
CHUNK = 512
NCHUNK = T // CHUNK
CT = CHUNK // P
SEQ = T // BATCH
C = 128
DIN = 256
ND = DIN // P
NS = 16
TAPS = 4
PAD = TAPS - 1
R = 64
E0, F0 = 8, 512
E1, H1 = 16, 256
FK0, FK1 = F0 // P, H1 // P
ST0 = (2 * T + E0 * (P - 1)) // P
ST0 += ST0 % 2
ST1 = (2 * T + E1 * (P - 1)) // P
ST1 += -ST1 % 4
GT = 4
NG = ST1 // GT
LN_EPS = 1e-5
RMS_EPS1 = 1e-5
RMS_EPS2 = 1e-6
BIG = 64.0
LOWEST = -3.0e38
MAGIC = 1.5 * 2.0 ** 23
TURN = 6.283185
PI = 3.141592653589793
SA, CA, GA, SB, CB, GB = range(6)
TP, BC_BANK, Y_BANK = 0, 5, 6


def columns(widths):
    at, out = 0, {}
    for name, w in widths:
        out[name] = slice(at, at + w)
        at += w
    return out, at


V, NVEC = columns([("conv", ND * TAPS), ("convb", ND), ("bdt", ND), ("alog", ND * NS), ("dskip", ND),
                   ("c", 2 * BATCH), ("rmsw", 1), ("ba", 1), ("rw0", E0), ("rw1", E1)])
K, NCONST = columns([("ident", P), ("tri", P), ("sel", 2 * NS), ("eiota", E1), ("jiota", ST1),
                     ("reset", E1 * NTILE)])


def adaln_two_layers(nc, x, consts, vecs, w_in, conv_rows, w_x, w_dt, w_out, w1, b1, w2, b2, wmod,
                     w4, wo, mf, phase, down, norm_w, rbias1, out):
    slots_in = [nc.dram_tensor(f"slots_in{l}", (n * P, C), F32, kind="Internal").ap()
                for l, n in enumerate((ST0, ST1))]
    slots_out = [nc.dram_tensor(f"slots_out{l}", (n * P, C), F32, kind="Internal").ap()
                 for l, n in enumerate((ST0, ST1))]
    x_rows = x.rearrange("(t p) c -> p t c", p=P)
    out_rows = out.rearrange("(t p) c -> p t c", p=P)

    ctx = ExitStack()
    with ctx:
        start_at = 16512
        top = [start_at]

        def place(name, shape, dt=F32, at=None):
            size = 2 if dt == BF16 else 4
            for s in shape[1:]:
                size *= s
            begin = top[0] if at is None else at
            end = begin + (size + 31) // 32 * 32
            if at is None:
                top[0] = end
            assert end <= 229344, (name, end)
            return nc.alloc_sbuf_tensor_at(name, shape, dt, offset=begin), end

        def put(name, shape, dt=F32):
            return place(name, shape, dt)[0]

        def sem(name):
            return ctx.enter_context(nc.semaphore(name))

        x_tok = put("x_tok", [P, NTILE, C])
        h_at = top[0]
        h_tok = put("h_tok", [P, NTILE, C])
        hT_at = top[0]
        hT = put("hT", [P, BATCH, PAD + SEQ])
        cst = put("cst", [P, NCONST])
        vec = put("vec", [P, NVEC])
        mod = put("mod", [P, 2, BATCH, 6, C])
        tri_b = put("tri_b", [P, P], BF16)
        ones_b = put("ones_b", [P, P], BF16)
        ones_f = put("ones_f", [P, E1])
        stats = put("stats", [P, CT, 6])
        ln_sum = put("ln_sum", [P, CT])
        ln_dif = put("ln_dif", [P, CT])
        ln_m2 = put("ln_m2", [P, CT])
        ln_mean = put("ln_mean", [P, CT])
        ln_rs = put("ln_rs", [P, CT])
        NRT = 9
        route = put("route", [P, NRT, E1 * NTILE])
        mask_b = put("mask_b", [P, E1 * NTILE], BF16)
        m12 = put("m12", [P, 2, NTILE])
        low = put("low", [P, NTILE])
        ssum = put("ssum", [P, NTILE])
        slot_f = put("slot_f", [P, NTILE])
        slot_i = put("slot_i", [P, 2, NTILE], I32)
        wts = put("wts", [P, 2, NTILE])
        tiles_e = put("tiles_e", [P, 4, E1])
        tile_f = put("tile_f", [P, ST1])
        tile_i = put("tile_i", [P, 2, ST1], I32)
        sc_wide = put("sc_wide", [P, 2 * BATCH, P])
        eps_s = put("eps_s", [P, 2])
        neg_a = put("neg_a", [P, ND, NS])
        hR = put("hR", [P, CHUNK])
        nw_s = put("nw_s", [P, C])
        rb1_s = put("rb1_s", [P, E1])
        xcmp = put("xcmp", [1, ST1 * E1])
        f0_at = top[0]

        w1_s, e = place("w1_s", [P, E0, F0], at=f0_at)
        b1_s, e = place("b1_s", [P, E0, F0], at=e)
        w2_s, e = place("w2_s", [P, E0, FK0, C], at=e)
        b2_s, m_at = place("b2_s", [P, E0, C], at=e)
        aT, e = place("aT", [P, T], at=f0_at)
        bT, e = place("bT", [P, T], at=e)
        sideT, e = place("sideT", [P, T], at=e)
        gateT, e = place("gateT", [P, T], at=e)
        scanT, e = place("scanT", [P, T], at=e)
        w4_s, e = place("w4_s", [P, 4, C], at=e)
        wo_s, e = place("wo_s", [P, C], at=e)
        wo_g, e = place("wo_g", [P, BATCH, C], at=e)
        rms_ss, e = place("rms_ss", [P, NTILE], at=e)
        rms_sq, e = place("rms_sq", [P, CT, C], at=e)
        xn_tok, e = place("xn_tok", [P, CT, C], at=e)
        assert e <= m_at
        freq, e = place("freq", [P, ST1, H1], at=f0_at)
        assert e <= m_at
        y1 = [None, None]
        y1[0], e = place("y1a", [P, NTILE, C], at=f0_at)
        y1[1], e = place("y1b", [P, NTILE, C], at=e)
        o1, e = place("o1", [P, NTILE, C], at=e)
        o1sq, e = place("o1sq", [P, NTILE, C], at=e)
        assert e <= m_at

        win_s, e = place("win_s", [P, 2 * DIN], at=m_at)
        convr_s, e = place("convr_s", [P, TAPS, DIN], at=e)
        wconv, e = place("wconv", [P, TAPS, DIN], at=e)
        wx_s, e = place("wx_s", [P, ND, R + 2 * NS], at=e)
        wdt_s, e = place("wdt_s", [R, DIN], at=e)
        wout_s, e = place("wout_s", [P, ND, C], at=e)
        wout_g, e = place("wout_g", [P, BATCH, ND, C], at=e)
        diag_d, e = place("diag_d", [P, ND, P], at=e)
        sel_b, e = place("sel_b", [3 * 2 * NS, 2 * NS, P], BF16, at=e)
        wmod_s, _ = place("wmod_s", [P, 2, 6 * C], at=e)
        xcT, e = place("xcT", [P, 2, ND, CHUNK], at=e)
        zsT, e = place("zsT", [P, 2, ND, CHUNK], at=e)
        dtlow, e = place("dtlow", [R, CHUNK], at=e)
        bc3, e = place("bc3", [3 * 2 * NS, CHUNK], BF16, at=e)
        bc_hi, e = place("bc_hi", [2 * NS, CHUNK], BF16, at=e)
        bc_rest, e = place("bc_rest", [2 * NS, CHUNK], at=e)
        softp, e = place("softp", [P, ND, CHUNK], at=e)
        dtT, e = place("dtT", [P, ND, CHUNK], at=e)
        uT, e = place("uT", [P, ND, CHUNK], at=e)
        b_sb, e = place("b_sb", [P, 2, CHUNK], at=e)
        bu, e = place("bu", [P, 2, ND, CHUNK], at=e)
        hs, e = place("hs", [P, 2, ND, CHUNK], at=e)
        prod, e = place("prod", [P, 2, ND, CHUNK], at=e)
        carry, e = place("carry", [P, ND, NS], at=e)
        yT, e = place("yT", [P, ND, CHUNK], at=e)
        m_end = e
        mf_s, e = place("mf_s", [P, E1, 2 * H1], at=m_at)
        phase_s, e = place("phase_s", [P, E1, H1], at=e)
        w_end = e
        down_s, e = place("down_s", [P, E1, FK1, C], at=w_end - E1 * H1 * 4)
        assert e <= w_end
        xl0, e = place("xl0", [P, 2, C], at=w_end)
        xt0, e = place("xt0", [P, 2, P], at=e)
        hp0, e = place("hp0", [P, 2, F0], at=e)
        ht0, e = place("ht0", [P, 2, F0], at=e)
        ys0, e = place("ys0", [P, 2, C], at=e)
        y0 = [None, None]
        y0[0], e = place("y0a", [P, NTILE, C], at=e)
        y0[1], e = place("y0b", [P, NTILE, C], at=e)
        mag, e = place("mag", [P, ST1, H1], at=w_end)
        xl1, e = place("xl1", [P, 2, C], at=h_at)
        xt1, e = place("xt1", [P, 2, P], at=e)
        hd1, e = place("hd1", [P, 2, H1], at=e)
        ht1, e = place("ht1", [P, 2, H1], at=e)
        ys1, e = place("ys1", [P, 2, C], at=e)
        assert e <= hT_at
        fabs, e = place("fabs", [P, 2, GT, H1], at=hT_at)
        hold = route[:, 0:4, :].rearrange("p a (k h) -> p a k h", k=1).rearrange("p (q a) k h -> p q (a k) h", q=1)
        zero_s, _ = place("zero_s", [P, 6 * C], at=m_end - 6 * C * 4)

        ps = ctx.enter_context(nc.psum_tensor("ps", [P, 8, CHUNK], F32))

        def bank(b, n=1):
            return ps[:, b, :] if n == 1 else ps[:, b:b + n, :]

        ident = cst[:, K["ident"]]
        conv_b, b_dt, d_skip = vec[:, V["convb"]], vec[:, V["bdt"]], vec[:, V["dskip"]]

        names = ("in_small in_x in_wmod in_ssm in_w1 in_l1 in_nw in_phase in_down zeros_set zeroed mod_silu mod_ps mod_done "
                 "consts_b ln_stats ln_rstd h_ready hT_ps hT_sb conv_ps z_ps xc_ready zs_ready dbl_ps dtlow_sb "
                 "bc3_ready dt_ps softp_done dt_ready b_ps b_copied c_ps a_ready bu_ready scan_done prod_ready "
                 "sum_done y_ready o_ps x_added logit_ps logit_sb wts_ready neg_ready pad_zeroed "
                 "mask_ready rank_ps pick_exp pick_exp_done slots_ready scattered "
                 "xt_ps0 xt_sb0 up_ps0 up_sb0 ht_ps0 ht_sb0 dn_ps0 dn_sb0 gathered0 "
                 "rms_sum rms_rstd xn_ready p4_ps p4_a p4_side p4_gate gated_y b_gated carried whole1 res_ready in_f1 "
                 "xt_ps1 xt_sb1 up_ps1 up_abs1 up_sb1 soft_e1 soft_l1 added1 theta1 turned1 cos1 tanh1 hid1 ht_ps1 ht_sb1 dn_ps1 dn_sb1 gathered1 "
                 "o_mix o_rstd o_final stored act_chain dve_chain pool_chain phase_done w_scaled").split()
        S = {n: sem(n) for n in names}
        loaded = {(l, u): sem(f"slot_loaded{l}_{u}") for l in range(2) for u in range(2)}
        saved = {(l, u): sem(f"slot_saved{l}_{u}") for l in range(2) for u in range(2)}

        block = ctx.enter_context(nc.Block())

        @block.sync
        def _(sp):
            sp.dma_start(vec[:, :], vecs).then_inc(S["in_small"], 16)
            sp.dma_start(cst[:, :], consts).then_inc(S["in_small"], 16)
            for c in range(NCHUNK):
                sp.dma_start(x_tok[:, c * CT:(c + 1) * CT, :], x_rows[:, c * CT:(c + 1) * CT, :]).then_inc(S["in_x"], 16)
            sp.dma_start(wmod_s[:, :, :], wmod).then_inc(S["in_wmod"], 16)
            for dst, src in ((win_s[:, :], w_in), (convr_s[:, :, :], conv_rows.partition_broadcast(P)),
                             (wx_s[:, :, :], w_x), (wdt_s[:, :], w_dt), (wout_s[:, :, :], w_out)):
                sp.dma_start(dst, src).then_inc(S["in_ssm"], 16)
            sp.dma_start(w1_s[:, :, :], w1).then_inc(S["in_w1"], 16)
            sp.dma_start(b1_s[:, :, :], b1.partition_broadcast(P)).then_inc(S["in_w1"], 16)
            sp.dma_start(w2_s[:, :, :, :], w2).then_inc(S["in_w1"], 16)
            sp.dma_start(b2_s[:, :, :], b2.partition_broadcast(P)).then_inc(S["in_w1"], 16)
            sp.dma_start(nw_s[:, :], norm_w.partition_broadcast(P)).then_inc(S["in_nw"], 16)
            sp.dma_start(rb1_s[:, :], rbias1.partition_broadcast(P)).then_inc(S["in_nw"], 16)
            sp.wait_ge(S["zeros_set"], 1)
            for l, n in enumerate((ST0, ST1)):
                rows = slots_in[l].rearrange("(p a) c -> p (a c)", p=P)
                at = 0
                while at < n:
                    k = min(6, n - at)
                    sp.dma_start(rows[:, at * C:(at + k) * C], zero_s[:, 0:k * C]).then_inc(S["zeroed"], 16)
                    at += k
            sp.wait_ge(S["x_added"], NCHUNK)
            sp.dma_start(mf_s[:, :, :], mf).then_inc(S["in_f1"], 16)
            sp.dma_start(phase_s[:, :, :], phase.partition_broadcast(P)).then_inc(S["in_phase"], 16)

            def slot_loads(l, n, xl):
                sp.wait_ge(S["scattered"], 16 * 2 * NTILE * (l + 1))
                with sp.Fori(0, n // 2) as i:
                    for u in range(2):
                        sp.wait_ge(S[f"xt_ps{l}"], i * 2 + (u + 1))
                        sp.dma_start(xl[:, u, :], slots_in[l][bass.ds(i * (2 * P) + u * P, P), :]).then_inc(loaded[l, u], 16)

            sp.sem_inc(S["xt_ps0"], 2)
            slot_loads(0, ST0, xl0)
            sp.wait_ge(S["dn_sb0"], ST0 + 2)
            sp.dma_start(w4_s[:, :, :], w4).then_inc(S["in_l1"], 16)
            sp.dma_start(wo_s[:, :], wo).then_inc(S["in_l1"], 16)
            sp.sem_inc(S["xt_ps1"], 2)
            slot_loads(1, ST1, xl1)
            sp.wait_ge(S["up_sb1"], ST1 + GT)
            sp.dma_start(down_s[:, :, :, :], down).then_inc(S["in_down"], 16)
            for c in range(NCHUNK):
                sp.wait_ge(S["o_final"], c + 1)
                sp.dma_start(out_rows[:, c * CT:(c + 1) * CT, :], x_tok[:, c * CT:(c + 1) * CT, :]).then_inc(S["stored"], 16)
            sp.wait_ge(S["stored"], 16 * NCHUNK)

        @block.gpsimd
        def _(pool):
            def scatter(l):
                pool.wait_ge(S["slots_ready"], l + 1)
                pool.wait_ge(S["zeroed"], 16 * (-(-ST0 // 6) + -(-ST1 // 6)))
                for t in range(NTILE):
                    for k in range(2):
                        pool.indirect_dma_start(slots_in[l], bass.IndirectOffsetOnAxis(ap=slot_i[:, k, t:t + 1], axis=0),
                                                h_tok[:, t, :], None).then_inc(S["scattered"], 16)

            def gather(l, n, y):
                for u in range(2):
                    pool.wait_ge(saved[l, u], 16 * (n // 2))
                for t in range(NTILE):
                    for k in range(2):
                        pool.indirect_dma_start(y[k][:, t, :], None, slots_out[l],
                                                bass.IndirectOffsetOnAxis(ap=slot_i[:, k, t:t + 1], axis=0)
                                                ).then_inc(S[f"gathered{l}"], 16)

            def save(l, n, ys):
                with pool.Fori(0, n // 2) as i:
                    for u in range(2):
                        pool.wait_ge(S[f"dn_sb{l}"], i * 2 + (u + 3))
                        pool.dma_start(slots_out[l][bass.ds(i * (2 * P) + u * P, P), :], ys[:, u, :]).then_inc(saved[l, u], 16)

            pool.memset(ones_b[:, :], 1.0).then_inc(S["consts_b"], 1)
            pool.memset(ones_f[:, :], 1.0).then_inc(S["consts_b"], 1)
            pool.memset(eps_s[:, 0:1], LN_EPS).then_inc(S["consts_b"], 1)
            pool.memset(eps_s[:, 1:2], RMS_EPS2).then_inc(S["consts_b"], 1)
            pool.memset(zero_s[:, :], 0.0).then_inc(S["zeros_set"], 1)
            pool.memset(hT[:, :, 0:PAD], 0.0).then_inc(S["pad_zeroed"], 1)
            pool.sem_inc(S["bu_ready"], 2)
            for c in range(NCHUNK):
                pool.wait_ge(S["dt_ready"], 2 * c + 2)
                with pool.Fori(0, NS // 2) as i:
                    for k in range(2):
                        g = i * 2 + (c * NS + k)
                        pool.wait_ge(S["b_copied"], g + 2)
                        pool.wait_ge(S["scan_done"], g * 2 + 2)
                        nc.gpsimd.tensor_tensor(bu[:, k, :, :], uT[:, :, :],
                                                b_sb[:, k:k + 1, :].broadcast_to([P, ND, CHUNK]),
                                                ALU.mult).then_inc(S["bu_ready"], 1)
            scatter(0)
            save(0, ST0, ys0)
            gather(0, ST0, y0)
            pool.wait_ge(S["in_phase"], 16)
            nc.gpsimd.tensor_scalar(phase_s[:, :, :], phase_s[:, :, :], 0.1, PI / 2, ALU.add, ALU.add).then_inc(S["phase_done"], 1)
            for c in range(NCHUNK):
                ts = slice(c * CT, (c + 1) * CT)
                pool.wait_ge(S["xn_ready"], c + 1)
                pool.wait_ge(S["rms_sum"], c + 1)
                ga = mod[:, 1, c // 2, GA, :].unsqueeze(1).broadcast_to([P, CT, C])
                nc.gpsimd.tensor_tensor(h_tok[:, ts, :], h_tok[:, ts, :], ga, ALU.mult).then_inc(S["res_ready"], 1)
            scatter(1)
            for g in range(NG):
                gs = slice(g * GT, (g + 1) * GT)
                pool.wait_ge(S["soft_l1"], g + 1)
                pool.wait_ge(S["up_sb1"], GT * (g + 2))
                nc.gpsimd.tensor_tensor(freq[:, gs, :], freq[:, gs, :], fabs[:, g % 2, :, :], ALU.add).then_inc(S["added1"], 1)
                pool.wait_ge(S["added1"], g + 1)
                nc.gpsimd.tensor_scalar(freq[:, gs, :], freq[:, gs, :], 1.0 / (2 * PI), None, ALU.mult).then_inc(S["theta1"], 1)
            save(1, ST1, ys1)
            gather(1, ST1, y1)

        @block.scalar
        def _(act):
            chain = [0]

            def then(ins):
                chain[0] += 1
                ins.then_inc(S["act_chain"], 1)
                act.wait_ge(S["act_chain"], chain[0])

            LOG_EXP, SILU_TANH_SIN, SIGMOID = "natural_log_exp_and_others", "silu_and_others", "sigmoid_and_others"

            def rstd(s, c):
                act.wait_ge(S["ln_stats"], s * NCHUNK + c + 1)
                then(nc.scalar.activation(ln_rs[:, :], ln_m2[:, :], ACT.Ln, bias=vec_eps(LN_EPS), scale=1.0 / C))
                nc.scalar.activation(ln_rs[:, :], ln_rs[:, :], ACT.Exp, scale=-0.5).then_inc(S["ln_rstd"], 1)

            def vec_eps(v):
                return eps_s[:, {LN_EPS: 0, RMS_EPS2: 1}[v]:{LN_EPS: 0, RMS_EPS2: 1}[v] + 1]

            act.wait_ge(S["in_small"], 32)
            act.wait_ge(S["consts_b"], 4)
            nc.scalar.activation(sc_wide[:, :, :], vec[:, V["c"]].unsqueeze(2).broadcast_to([P, 2 * BATCH, P]), ACT.Silu).then_inc(S["mod_silu"], 1)
            nc.scalar.activation(neg_a[:, :, :], vec[:, V["alog"]].rearrange("p (d n) -> p d n", d=ND), ACT.Exp).then_inc(S["neg_ready"], 1)
            act.preload_act_table_set(LOG_EXP)
            for c in range(NCHUNK):
                rstd(0, c)
            for c in range(NCHUNK):
                b, half = divmod(c, 2)
                act.wait_ge(S["hT_ps"], c + 1)
                act.wait_ge(S["pad_zeroed"], 1)
                nc.scalar.activation(hT[:, b, PAD + half * CHUNK:PAD + (half + 1) * CHUNK], bank(TP), ACT.Copy).then_inc(S["hT_sb"], 1)
            act.sem_inc(S["b_copied"], 1)
            act.wait_ge(S["neg_ready"], 2)
            for c in range(NCHUNK):
                q = c % 2
                act.preload_act_table_set(SILU_TANH_SIN)
                for d in range(ND):
                    act.wait_ge(S["conv_ps"], 2 * c + d + 1)
                    nc.scalar.activation(xcT[:, q, d, :], bank(1 + d), ACT.Silu, bias=conv_b[:, d:d + 1]).then_inc(S["xc_ready"], 1)
                for d in range(ND):
                    act.wait_ge(S["z_ps"], 2 * c + d + 1)
                    nc.scalar.activation(zsT[:, q, d, :], bank(3 + d), ACT.Silu).then_inc(S["zs_ready"], 1)
                act.wait_ge(S["dbl_ps"], c + 1)
                nc.scalar.activation(dtlow[:, :], ps[0:R, BC_BANK, :], ACT.Copy).then_inc(S["dtlow_sb"], 1)
                act.preload_act_table_set(LOG_EXP)
                for d in range(ND):
                    act.wait_ge(S["dt_ps"], 2 * c + d + 1)
                    nc.scalar.activation(dtT[:, d, :], bank(1 + d), ACT.Relu, bias=b_dt[:, d:d + 1])
                    then(nc.scalar.activation(softp[:, d, :], bank(1 + d), ACT.Abs, bias=b_dt[:, d:d + 1]))
                    then(nc.scalar.activation(softp[:, d, :], softp[:, d, :], ACT.Exp, scale=-1.0))
                    nc.scalar.activation(softp[:, d, :], softp[:, d, :], ACT.Ln, bias=1.0).then_inc(S["softp_done"], 1)
                def copy_b(g, k):
                    act.wait_ge(S["b_ps"], g + 1)
                    act.wait_ge(S["bu_ready"], g + 1)
                    nc.scalar.activation(b_sb[:, k, :], bank(BC_BANK), ACT.Copy).then_inc(S["b_copied"], 1)

                def decay(g, n, k):
                    for d in range(ND):
                        act.wait_ge(S["scan_done"], g * 2 + (d + 1))
                        nc.scalar.activation(bank(1 + 2 * k + d), dtT[:, d, :], ACT.Exp,
                                             scale=neg_a[:, d, bass.ds(n, 1)]).then_inc(S["a_ready"], 1)

                copy_b(c * NS, 0)
                copy_b(c * NS + 1, 1)
                act.wait_ge(S["dt_ready"], 2 * c + 2)
                decay(c * NS, 0, 0)
                with act.Fori(0, NS // 2 - 1) as i:
                    for k in range(2):
                        g = i * 2 + (c * NS + k)
                        decay(g + 1, i * 2 + (k + 1), 1 - k)
                        copy_b(g + 2, k)
                decay(c * NS + NS - 1, NS - 1, 1)
                rstd(1, c)
                act.wait_ge(S["hT_ps"], NCHUNK + c + 1)
                nc.scalar.activation(hR[:, :], bank(TP), ACT.Copy).then_inc(S["hT_sb"], 1)
            act.wait_ge(S["pick_exp"], 1)
            nc.scalar.activation(route[:, 8, 0:E0 * NTILE], route[:, 8, 0:E0 * NTILE], ACT.Exp).then_inc(S["pick_exp_done"], 1)
            act.sem_inc(S["xt_sb0"], 2)
            act.sem_inc(S["ht_sb0"], 2)

            def copy_xt(l, xt, j, u):
                act.wait_ge(S[f"xt_ps{l}"], j + 3)
                act.wait_ge(S[f"up_ps{l}"], j + 1)
                nc.scalar.activation(xt[:, u, :], ps[:, u, 0:P], ACT.Copy).then_inc(S[f"xt_sb{l}"], 1)

            def relu_ht(j, u):
                act.wait_ge(S["ht_ps0"], j + 3)
                act.wait_ge(S["dn_ps0"], j + 1)
                nc.scalar.activation(ht0[:, u, :], bank(4 + u), ACT.Relu).then_inc(S["ht_sb0"], 1)

            copy_xt(0, xt0, 0, 0)
            copy_xt(0, xt0, 1, 1)
            with act.Fori(0, (ST0 - 2) // 2) as i:
                for u in range(2):
                    copy_xt(0, xt0, i * 2 + (u + 2), u)
                    relu_ht(i * 2 + u, u)
            relu_ht(ST0 - 2, 0)
            relu_ht(ST0 - 1, 1)
            for c in range(NCHUNK):
                act.preload_act_table_set(LOG_EXP)
                rstd(2, c)
                act.wait_ge(S["h_ready"], 2 * NCHUNK + c + 1)
                for t in range(CT):
                    then(nc.scalar.activation(rms_sq[:, t, :], h_tok[:, c * CT + t, :], ACT.Square,
                                              accum_out=rms_ss[:, c * CT + t:c * CT + t + 1]))
                ss = rms_ss[:, c * CT:(c + 1) * CT]
                then(nc.scalar.activation(ss, ss, ACT.Ln, bias=vec_eps(RMS_EPS1), scale=1.0 / C))
                nc.scalar.activation(ss, ss, ACT.Exp, scale=-0.5).then_inc(S["rms_sum"], 1)
                act.wait_ge(S["hT_ps"], 2 * NCHUNK + c + 1)
                nc.scalar.activation(hR[:, :], bank(TP), ACT.Copy).then_inc(S["hT_sb"], 1)
                cs = slice(c * CHUNK, (c + 1) * CHUNK)
                act.preload_act_table_set(SIGMOID)
                act.wait_ge(S["p4_ps"], 4 * c + 1)
                nc.scalar.activation(aT[:, cs], bank(1), ACT.Sigmoid, bias=vec[:, V["ba"]]).then_inc(S["p4_a"], 1)
                act.wait_ge(S["p4_ps"], 4 * c + 3)
                nc.scalar.activation(sideT[:, cs], bank(3), ACT.Sigmoid).then_inc(S["p4_side"], 1)
                act.wait_ge(S["p4_ps"], 4 * c + 4)
                nc.scalar.activation(gateT[:, cs], bank(4), ACT.Sigmoid).then_inc(S["p4_gate"], 1)
            act.preload_act_table_set(LOG_EXP)
            for c in range(NCHUNK):
                rstd(3, c)
                act.wait_ge(S["hT_ps"], 3 * NCHUNK + c + 1)
                nc.scalar.activation(hR[:, :], bank(TP), ACT.Copy).then_inc(S["hT_sb"], 1)
            act.wait_ge(S["pick_exp"], 2)
            nc.scalar.activation(route[:, 8, 0:NTILE], route[:, 8, 0:NTILE], ACT.Exp).then_inc(S["pick_exp_done"], 1)

            act.sem_inc(S["xt_sb1"], 2)
            act.sem_inc(S["theta1"], 2)
            copy_xt(1, xt1, 0, 0)

            def group_abs(g, q, last):
                act.wait_ge(S["theta1"], g + 1)
                for k in range(GT):
                    j = g * GT + k
                    if not (last and k == GT - 1):
                        copy_xt(1, xt1, j + 1, (k + 1) % 2)
                    act.wait_ge(S["up_ps1"], j + 3)
                    nc.scalar.activation(fabs[:, q, k, :], ps[:, 2 + k, H1:2 * H1], ACT.Abs).then_inc(S["up_abs1"], 1)
                act.wait_ge(S["up_abs1"], g * GT + GT)
                nc.scalar.activation(fabs[:, q, :, :], fabs[:, q, :, :], ACT.Exp, scale=-1.0).then_inc(S["soft_e1"], 1)
                act.wait_ge(S["soft_e1"], g + 1)
                nc.scalar.activation(fabs[:, q, :, :], fabs[:, q, :, :], ACT.Ln, bias=1.0).then_inc(S["soft_l1"], 1)

            with act.Fori(0, NG // 2 - 1) as i:
                for q in range(2):
                    group_abs(i * 2 + q, q, False)
            group_abs(NG - 2, 0, False)
            group_abs(NG - 1, 1, True)
            act.preload_act_table_set(SILU_TANH_SIN)
            act.wait_ge(S["turned1"], NG + 1)
            with act.Fori(0, NG) as g:
                gs = bass.ds(g * GT, GT)
                nc.scalar.activation(mag[:, gs, :], mag[:, gs, :], ACT.Tanh).then_inc(S["tanh1"], 1)
                nc.scalar.activation(freq[:, gs, :], freq[:, gs, :], ACT.Sin, scale=TURN).then_inc(S["cos1"], 1)
            act.preload_act_table_set(LOG_EXP)
            act.wait_ge(S["o_mix"], 1)
            for t in range(NTILE):
                then(nc.scalar.activation(o1sq[:, t, :], o1[:, t, :], ACT.Square, accum_out=ssum[:, t:t + 1]))
            then(nc.scalar.activation(ssum[:, :], ssum[:, :], ACT.Ln, bias=vec_eps(RMS_EPS2), scale=1.0 / C))
            nc.scalar.activation(ssum[:, :], ssum[:, :], ACT.Exp, scale=-0.5).then_inc(S["o_rstd"], 1)

        @block.tensor
        def _(pe):
            def transposes(s, c):
                src = xn_tok if s == 2 else h_tok
                pe.wait_ge(S["xn_ready"] if s == 2 else S["h_ready"], c + 1 if s == 2 else s * NCHUNK + c + 1)
                if c or s:
                    pe.wait_ge(S["hT_sb"], s * NCHUNK + c)
                for t in range(CT):
                    last = nc.tensor.transpose(ps[:, TP, t * P:(t + 1) * P], src[:, t if s == 2 else c * CT + t, :], ident)
                last.then_inc(S["hT_ps"], 1)

            def logits(l, c, e):
                pe.wait_ge(S["hT_sb"], (2 * l + 1) * NCHUNK + c + 1)
                for t in range(CT):
                    last = nc.tensor.matmul(ps[:, BC_BANK, t * E1:t * E1 + e], hR[:, t * P:(t + 1) * P],
                                            vec[:, V[f"rw{l}"]], start=True, stop=True)
                last.then_inc(S["logit_ps"], 1)

            def ranks(l, e):
                pe.wait_ge(S["mask_ready"], l + 1)
                n = e * NTILE
                nc.tensor.matmul(ps[:, 1, 0:n], tri_b[:, :], mask_b[:, 0:n], start=True, stop=True)
                nc.tensor.matmul(ps[:, 2, 0:n], ones_b[:, :], mask_b[:, 0:n], start=True, stop=True).then_inc(S["rank_ps"], 1)

            pe.wait_ge(S["mod_silu"], 1)
            pe.wait_ge(S["in_wmod"], 16)
            pe.wait_ge(S["in_small"], 32)
            for lb, (q0, q1) in enumerate(((1, 2), (3, 4), (5, 6), (7, 0))):
                w = wmod_s[:, lb // BATCH, :]
                nc.tensor.matmul(bank(q0), sc_wide[:, lb, :], w[:, 0:CHUNK], start=True, stop=True)
                nc.tensor.matmul(ps[:, q1, 0:2 * C], sc_wide[:, lb, :], w[:, CHUNK:6 * C], start=True, stop=True).then_inc(S["mod_ps"], 1)
            pe.wait_ge(S["mod_done"], 1)
            for c in range(NCHUNK):
                transposes(0, c)
            pe.wait_ge(S["w_scaled"], 1)
            pe.sem_inc(S["sum_done"], 2)
            for c in range(NCHUNK):
                b, half = divmod(c, 2)
                q = c % 2
                lo = half * CHUNK
                pe.wait_ge(S["hT_sb"], NCHUNK if c == 0 else NCHUNK + c)
                for d in range(ND):
                    for k in range(TAPS):
                        last = nc.tensor.matmul(bank(1 + d), wconv[:, k, d * P:(d + 1) * P], hT[:, b, lo + k:lo + k + CHUNK],
                                                start=k == 0, stop=k == TAPS - 1)
                    last.then_inc(S["conv_ps"], 1)
                for d in range(ND):
                    nc.tensor.matmul(bank(3 + d), win_s[:, DIN + d * P:DIN + (d + 1) * P], hT[:, b, lo + PAD:lo + PAD + CHUNK],
                                     start=True, stop=True).then_inc(S["z_ps"], 1)
                pe.wait_ge(S["xc_ready"], 2 * c + 2)
                if c:
                    pe.wait_ge(S["logit_sb"], c)
                for d in range(ND):
                    last = nc.tensor.matmul(ps[0:R + 2 * NS, BC_BANK, :], wx_s[:, d, :], xcT[:, q, d, :], start=d == 0, stop=d == ND - 1)
                last.then_inc(S["dbl_ps"], 1)
                pe.wait_ge(S["dtlow_sb"], c + 1)
                for d in range(ND):
                    nc.tensor.matmul(bank(1 + d), wdt_s[:, d * P:(d + 1) * P], dtlow[:, :], start=True, stop=True).then_inc(S["dt_ps"], 1)
                for d in range(ND):
                    nc.tensor.matmul(bank(Y_BANK + d), diag_d[:, d, :], xcT[:, q, d, :], start=True, stop=False)

                def state_row(n):
                    return sel_b[:, bass.ds(n, 1), :].rearrange("p a m -> p (a m)")

                def b_row(g, n):
                    pe.wait_ge(S["b_copied"], g + 1)
                    nc.tensor.matmul(bank(BC_BANK), state_row(n), bc3[:, :], start=True, stop=True).then_inc(S["b_ps"], 1)

                def c_row(g, n):
                    nc.tensor.matmul(bank(TP), state_row(n), bc3[:, :], start=True, stop=True).then_inc(S["c_ps"], 1)

                def add_state(g, k, stop=False):
                    for d in range(ND):
                        last = nc.tensor.matmul(bank(Y_BANK + d), ident, prod[:, k, d, :], start=False, stop=stop)
                    last.then_inc(S["sum_done"], 1)

                pe.wait_ge(S["bc3_ready"], c + 1)
                g0 = c * NS
                for n in range(3):
                    b_row(g0 + n, n)
                    if n == 0:
                        c_row(g0, NS)
                with pe.Fori(0, NS // 2 - 2) as i:
                    for k in range(2):
                        g = i * 2 + (g0 + k)
                        pe.wait_ge(S["prod_ready"], g + 1)
                        c_row(g + 1, i * 2 + (k + 1 + NS))
                        b_row(g + 3, i * 2 + (k + 3))
                        add_state(g, k)
                for n in range(NS - 4, NS):
                    pe.wait_ge(S["prod_ready"], g0 + n + 1)
                    if n + 1 < NS:
                        c_row(g0 + n + 1, NS + n + 1)
                    if n + 3 < NS:
                        b_row(g0 + n + 3, n + 3)
                    add_state(g0 + n, n % 2, stop=n == NS - 1)
                pe.wait_ge(S["y_ready"], c + 1)
                for t in range(CT):
                    for d in range(ND):
                        last = nc.tensor.matmul(ps[:, BC_BANK, t * P:(t + 1) * P], yT[:, d, t * P:(t + 1) * P],
                                                wout_g[:, b, d, :], start=d == 0, stop=d == ND - 1)
                last.then_inc(S["o_ps"], 1)
                transposes(1, c)
                pe.wait_ge(S["x_added"], c + 1)
                logits(0, c, E0)
            ranks(0, E0)


            def at(j):
                return slice(j, j + 1) if isinstance(j, int) else bass.ds(j, 1)

            def expert_of(l, j, n):
                return pe.value_load(tile_i[0:1, l, at(j)], min_val=0, max_val=n - 1)

            def turn_x(l, xl, j, j2, u):
                pe.wait_ge(loaded[l, u], j2 * 16 + 16)
                pe.wait_ge(S[f"xt_sb{l}"], j + 1)
                nc.tensor.transpose(ps[:, u, 0:P], xl[:, u, :], ident).then_inc(S[f"xt_ps{l}"], 1)

            def up0(j, u):
                e = expert_of(0, j, E0)
                pe.wait_ge(S["xt_sb0"], j + 3)
                pe.wait_ge(S["up_sb0"], j + 1)
                nc.tensor.matmul(bank(2 + u), xt0[:, u, :], w1_s[:, bass.ds(e, 1), :].rearrange("p a f -> p (a f)"),
                                 start=True, stop=True).then_inc(S["up_ps0"], 1)

            def turn_h0(j, u):
                pe.wait_ge(S["up_sb0"], j + 3)
                pe.wait_ge(S["ht_sb0"], j + 1)
                for k in range(FK0):
                    last = nc.tensor.transpose(ps[:, 4 + u, k * P:(k + 1) * P], hp0[:, u, k * P:(k + 1) * P], ident)
                last.then_inc(S["ht_ps0"], 1)

            def down_rows(l, j, u, n, fk, ht, w, e_n):
                e = expert_of(l, j, e_n)
                pe.wait_ge(S[f"ht_sb{l}"], j + 3)
                pe.wait_ge(S[f"dn_sb{l}"], j + 1)
                for k in range(fk):
                    last = nc.tensor.matmul(ps[:, 6 + u, 0:C], ht[:, u, k * P:(k + 1) * P],
                                            w[:, bass.ds(e, 1), k, :].rearrange("p a c -> p (a c)"), start=k == 0, stop=k == fk - 1)
                last.then_inc(S[f"dn_ps{l}"], 1)

            def down0(j, u):
                down_rows(0, j, u, ST0, FK0, ht0, w2_s, E0)

            pe.wait_ge(S["slots_ready"], 1)
            pe.wait_ge(S["in_w1"], 64)
            pe.sem_inc(S["up_ps0"], 2)
            pe.sem_inc(S["ht_ps0"], 2)
            pe.sem_inc(S["dn_ps0"], 2)
            turn_x(0, xl0, 0, 0, 0)
            turn_x(0, xl0, 1, 0, 1)
            up0(0, 0)
            turn_x(0, xl0, 2, 1, 0)
            up0(1, 1)
            turn_h0(0, 0)
            with pe.Fori(0, (ST0 - 4) // 2) as i:
                for k in range(2):
                    j = i * 2 + (k + 2)
                    turn_x(0, xl0, j + 1, i + (1 + (1 + k) // 2), 1 - k)
                    up0(j, k)
                    turn_h0(j - 1, 1 - k)
                    down0(j - 2, k)
            n = ST0
            turn_x(0, xl0, n - 1, n // 2 - 1, 1)
            up0(n - 2, 0)
            turn_h0(n - 3, 1)
            down0(n - 4, 0)
            up0(n - 1, 1)
            turn_h0(n - 2, 0)
            down0(n - 3, 1)
            turn_h0(n - 1, 1)
            down0(n - 2, 0)
            down0(n - 1, 1)
            pe.wait_ge(S["w_scaled"], 2)
            for c in range(NCHUNK):
                transposes(2, c)
                pe.wait_ge(S["hT_sb"], 2 * NCHUNK + c + 1)
                if c:
                    pe.wait_ge(S["p4_gate"], c)
                    pe.wait_ge(S["b_gated"], c)
                for m in range(4):
                    nc.tensor.matmul(bank(1 + m), w4_s[:, m, :], hR[:, :], start=True, stop=True).then_inc(S["p4_ps"], 1)
            for c in range(NCHUNK):
                pe.wait_ge(S["gated_y"], c + 1)
                for t in range(CT):
                    last = nc.tensor.matmul(ps[:, BC_BANK, t * P:(t + 1) * P], gateT[:, c * CHUNK + t * P:c * CHUNK + (t + 1) * P],
                                            wo_g[:, c // 2, :], start=True, stop=True)
                last.then_inc(S["o_ps"], 1)
                transposes(3, c)
                logits(1, c, E1)
                pe.wait_ge(S["logit_sb"], NCHUNK + c + 1)
            ranks(1, E1)
            pe.wait_ge(S["slots_ready"], 2)
            pe.wait_ge(S["in_f1"], 16)

            def up1(j, u):
                e = expert_of(1, j, E1)
                pe.wait_ge(S["xt_sb1"], j + 3)
                pe.wait_ge(S["up_sb1"], j + 1)
                nc.tensor.matmul(bank(2 + u), xt1[:, u % 2, :], mf_s[:, bass.ds(e, 1), :].rearrange("p a f -> p (a f)"),
                                 start=True, stop=True).then_inc(S["up_ps1"], 1)

            pe.sem_inc(S["up_ps1"], 2)
            turn_x(1, xl1, 0, 0, 0)
            with pe.Fori(0, ST1 // GT - 1) as i:
                for k in range(GT):
                    j = i * GT + k
                    turn_x(1, xl1, j + 1, i * 2 + (1 + k) // 2, 1 - k % 2)
                    up1(j, k)
            for j in range(ST1 - GT, ST1):
                if j + 1 < ST1:
                    turn_x(1, xl1, j + 1, (j + 1) // 2, 1 - j % 2)
                up1(j, j % GT)

            def turn_h1(j, u):
                pe.wait_ge(S["hid1"], j + 1)
                pe.wait_ge(S["ht_sb1"], j + 1)
                for k in range(FK1):
                    last = nc.tensor.transpose(ps[:, 4 + u, k * P:(k + 1) * P], hd1[:, u, k * P:(k + 1) * P], ident)
                last.then_inc(S["ht_ps1"], 1)

            def down1(j, u):
                down_rows(1, j, u, ST1, FK1, ht1, down_s, E1)

            pe.sem_inc(S["ht_ps1"], 2)
            pe.sem_inc(S["dn_ps1"], 2)
            turn_h1(0, 0)
            pe.wait_ge(S["in_down"], 16)
            with pe.Fori(0, (ST1 - 2) // 2) as i:
                for k in range(2):
                    turn_h1(i * 2 + (k + 1), 1 - k)
                    down1(i * 2 + k, k)
            turn_h1(ST1 - 1, 1)
            down1(ST1 - 2, 0)
            down1(ST1 - 1, 1)

        @block.vector
        def _(dve):
            chain = [0]

            def then(ins):
                chain[0] += 1
                ins.then_inc(S["dve_chain"], 1)
                dve.wait_ge(S["dve_chain"], chain[0])

            def norm_rows(s, c):
                l, m = s // 2, (SA, CA) if s % 2 == 0 else (SB, CB)
                for t in range(CT):
                    ins = nc.vector.bn_stats(stats[:, t, :], x_tok[:, c * CT + t, :])
                then(ins)
                col = lambda k: stats[:, :, k]
                nc.vector.tensor_tensor(ln_sum[:, :], col(1), col(4), ALU.add)
                nc.vector.tensor_tensor(ln_dif[:, :], col(1), col(4), ALU.subtract)
                then(nc.vector.tensor_tensor(ln_m2[:, :], col(2), col(5), ALU.add))
                nc.vector.tensor_scalar(ln_mean[:, :], ln_sum[:, :], 0.5, None, ALU.mult)
                then(nc.vector.tensor_tensor(ln_dif[:, :], ln_dif[:, :], ln_dif[:, :], ALU.mult))
                ins = nc.vector.scalar_tensor_tensor(out=ln_m2[:, :], in0=ln_dif[:, :], scalar=C / 4.0, in1=ln_m2[:, :],
                                                     op0=ALU.mult, op1=ALU.add)
                ins.then_inc(S["ln_stats"], 1)
                dve.wait_ge(S["ln_rstd"], s * NCHUNK + c + 1)
                for t in range(CT):
                    ins = nc.vector.tensor_scalar(h_tok[:, c * CT + t, :], x_tok[:, c * CT + t, :], ln_mean[:, t:t + 1],
                                                  ln_rs[:, t:t + 1], ALU.subtract, ALU.mult)
                then(ins)
                h = h_tok[:, c * CT:(c + 1) * CT, :]
                wide = lambda k: mod[:, l, c // 2, k, :].unsqueeze(1).broadcast_to([P, CT, C])
                then(nc.vector.tensor_tensor(h, h, wide(m[1]), ALU.mult))
                nc.vector.tensor_tensor(h, h, wide(m[0]), ALU.add).then_inc(S["h_ready"], 1)
                dve.wait_ge(S["h_ready"], s * NCHUNK + c + 1)

            def take_logits(l, c, e):
                dve.wait_ge(S["logit_ps"], l * NCHUNK + c + 1)
                src = ps[:, BC_BANK, 0:CT * E1].rearrange("p (t e) -> p t e", e=E1)[:, :, 0:e]
                dst = route[:, 0, 0:e * NTILE].rearrange("p (e t) -> p t e", t=NTILE)[:, c * CT:(c + 1) * CT, :]
                if l:
                    ins = nc.vector.tensor_tensor(dst, src, rb1_s[:, :].unsqueeze(1).broadcast_to([P, CT, e]), ALU.add)
                else:
                    ins = nc.vector.tensor_copy(dst, src)
                ins.then_inc(S["logit_sb"], 1)
                dve.wait_ge(S["logit_sb"], l * NCHUNK + c + 1)

            def pick(l, e_n, st):
                n = e_n * NTILE

                def et(r):
                    return route[:, r, 0:n].rearrange("p (e t) -> p e t", t=NTILE)

                def te(r):
                    return route[:, r, 0:n].rearrange("p (e t) -> p t e", t=NTILE)

                def over_e(a):
                    return a.unsqueeze(1).broadcast_to([P, e_n, NTILE])

                iota = cst[:, K["eiota"]][:, 0:e_n].unsqueeze(2).broadcast_to([P, e_n, NTILE])
                for k in range(2):
                    src, best = (0, m12[:, k, :]) if k == 0 else (3, m12[:, k, :])
                    then(nc.vector.tensor_reduce(best, te(src), axis=AX, op=ALU.max))
                    then(nc.vector.tensor_tensor(et(4), et(src), over_e(best), ALU.is_equal))
                    then(nc.vector.tensor_scalar(et(4), et(4), -BIG, BIG, ALU.mult, ALU.add))
                    then(nc.vector.tensor_tensor(et(4), et(4), iota, ALU.add))
                    then(nc.vector.tensor_reduce(low[:, :], te(4), axis=AX, op=ALU.min))
                    then(nc.vector.tensor_tensor(et(1 + k), iota, over_e(low[:, :]), ALU.is_equal))
                    if k == 0:
                        then(nc.vector.scalar_tensor_tensor(out=et(3), in0=et(1), scalar=LOWEST, in1=et(0), op0=ALU.mult, op1=ALU.add))
                nc.vector.tensor_tensor(mask_b[:, 0:n], route[:, 1, 0:n], route[:, 2, 0:n], ALU.add).then_inc(S["mask_ready"], 1)
                if l == 0:
                    nc.vector.tensor_tensor(et(8), et(0), over_e(m12[:, 0, :]), ALU.subtract).then_inc(S["pick_exp"], 1)
                else:
                    nc.vector.tensor_tensor(route[:, 8, 0:NTILE], m12[:, 1, :], m12[:, 0, :], ALU.subtract).then_inc(S["pick_exp"], 1)
                dve.wait_ge(S["rank_ps"], l + 1)
                then(nc.vector.tensor_copy(route[:, 4, 0:n], ps[:, 2, 0:n]))
                then(nc.vector.tensor_tensor_scan(route[:, 5, 0:n], cst[:, K["reset"]][:, 0:n], route[:, 4, 0:n], 0.0, ALU.mult, ALU.add))
                tot = route[:, 5, 0:n].rearrange("p (e t) -> p e t", t=NTILE)[:, :, NTILE - 1]
                then(nc.vector.tensor_scalar(tiles_e[:, 0, 0:e_n], tot, 1.0 / P, 0.5 - 0.5 / P, ALU.mult, ALU.add))
                then(nc.vector.tensor_scalar(tiles_e[:, 1, 0:e_n], tiles_e[:, 0, 0:e_n], MAGIC, MAGIC, ALU.add, ALU.subtract))
                then(nc.vector.tensor_tensor_scan(tiles_e[:, 2, 0:e_n], ones_f[:, 0:e_n], tiles_e[:, 1, 0:e_n], 0.0, ALU.mult, ALU.add))
                then(nc.vector.tensor_tensor(tiles_e[:, 3, 0:e_n], tiles_e[:, 2, 0:e_n], tiles_e[:, 1, 0:e_n], ALU.subtract))
                then(nc.vector.tensor_scalar(tiles_e[:, 3, 0:e_n], tiles_e[:, 3, 0:e_n], float(P), None, ALU.mult))
                then(nc.vector.tensor_tensor(route[:, 5, 0:n], route[:, 5, 0:n], route[:, 4, 0:n], ALU.subtract))
                then(nc.vector.tensor_tensor(route[:, 5, 0:n], route[:, 5, 0:n], ps[:, 1, 0:n], ALU.add))
                then(nc.vector.tensor_tensor(et(5), et(5), tiles_e[:, 3, 0:e_n].unsqueeze(2).broadcast_to([P, e_n, NTILE]), ALU.add))
                for k in range(2):
                    then(nc.vector.tensor_tensor(route[:, 4, 0:n], route[:, 1 + k, 0:n], route[:, 5, 0:n], ALU.mult))
                    then(nc.vector.tensor_reduce(slot_f[:, :], te(4), axis=AX, op=ALU.add))
                    then(nc.vector.tensor_copy(slot_i[:, k, :], slot_f[:, :]))
                cmp = xcmp[0:1, 0:st * e_n].rearrange("p (j e) -> p j e", e=e_n)
                then(nc.vector.tensor_tensor(cmp, cst[0:1, K["jiota"]][:, 0:st].unsqueeze(2).broadcast_to([1, st, e_n]),
                                             tiles_e[0:1, 2, 0:e_n].unsqueeze(1).broadcast_to([1, st, e_n]), ALU.is_ge))
                then(nc.vector.tensor_reduce(tile_f[0:1, 0:st], cmp, axis=AX, op=ALU.add))
                then(nc.vector.tensor_scalar(tile_f[0:1, 0:st], tile_f[0:1, 0:st], float(e_n - 1), None, ALU.min))
                nc.vector.tensor_copy(tile_i[0:1, l, 0:st], tile_f[0:1, 0:st]).then_inc(S["slots_ready"], 1)
                dve.wait_ge(S["slots_ready"], l + 1)
                dve.wait_ge(S["pick_exp_done"], l + 1)
                if l == 0:
                    then(nc.vector.tensor_reduce(ssum[:, :], te(8), axis=AX, op=ALU.add))
                    then(nc.vector.reciprocal(wts[:, 0, :], ssum[:, :]))
                    then(nc.vector.tensor_tensor(et(4), et(8), et(2), ALU.mult))
                    then(nc.vector.tensor_reduce(low[:, :], te(4), axis=AX, op=ALU.add))
                    then(nc.vector.tensor_tensor(wts[:, 1, :], low[:, :], wts[:, 0, :], ALU.mult))
                    then(nc.vector.tensor_tensor(low[:, :], wts[:, 0, :], wts[:, 1, :], ALU.add))
                    then(nc.vector.tensor_scalar(low[:, :], low[:, :], 1e-9, None, ALU.add))
                    then(nc.vector.reciprocal(low[:, :], low[:, :]))
                    then(nc.vector.tensor_tensor(wts[:, 0, :], wts[:, 0, :], low[:, :], ALU.mult))
                    then(nc.vector.tensor_tensor(wts[:, 1, :], wts[:, 1, :], low[:, :], ALU.mult))
                else:
                    ex = route[:, 8, 0:NTILE]
                    then(nc.vector.tensor_scalar(low[:, :], ex, 1.0, None, ALU.add))
                    then(nc.vector.reciprocal(wts[:, 0, :], low[:, :]))
                    then(nc.vector.tensor_tensor(wts[:, 1, :], ex, wts[:, 0, :], ALU.mult))

            dve.wait_ge(S["in_small"], 32)
            nc.vector.tensor_copy(tri_b[:, :], cst[:, K["tri"]]).then_inc(S["dve_chain"], 1)
            chain[0] += 1
            for lb, (q0, q1) in enumerate(((1, 2), (3, 4), (5, 6), (7, 0))):
                dve.wait_ge(S["mod_ps"], lb + 1)
                m = mod[:, lb // BATCH, lb % BATCH, :, :].rearrange("p k c -> p (k c)")
                nc.vector.tensor_copy(m[:, 0:CHUNK], bank(q0))
                ins = nc.vector.tensor_copy(m[:, CHUNK:6 * C], ps[:, q1, 0:2 * C])
            ins.then_inc(S["mod_done"], 1)
            dve.wait_ge(S["mod_done"], 1)
            every = mod[:, :, :, :, :].rearrange("p l b k c -> p (l b) k c")
            for k in (CA, CB):
                then(nc.vector.tensor_scalar(every[:, :, k, :], every[:, :, k, :], 1.0, None, ALU.add))
            for c in range(NCHUNK):
                dve.wait_ge(S["in_x"], 16 * (c + 1)) if c else dve.wait_ge(S["in_x"], 16 * NCHUNK)
                norm_rows(0, c)
            dve.wait_ge(S["in_ssm"], 80)
            nc.vector.tensor_tensor(wconv[:, :, :], win_s[:, 0:DIN].unsqueeze(1).broadcast_to([P, TAPS, DIN]), convr_s[:, :, :], ALU.mult)
            for d in range(ND):
                nc.vector.tensor_scalar(diag_d[:, d, :], ident, d_skip[:, d:d + 1], None, ALU.mult)
            nc.vector.tensor_copy(sel_b[:, :, :], cst[0:3 * 2 * NS, K["sel"]].unsqueeze(2).broadcast_to([3 * 2 * NS, 2 * NS, P])).then_inc(S["w_scaled"], 1)
            dve.wait_ge(S["neg_ready"], 1)
            nc.vector.tensor_scalar(neg_a[:, :, :], neg_a[:, :, :], -1.0, None, ALU.mult).then_inc(S["neg_ready"], 1)
            for k in (GA, GB):
                g = every[:, :, k, :]
                s0 = prod[:, 0, 0, :].rearrange("p (a c) -> p a c", a=4)
                s1 = prod[:, 0, 1, :].rearrange("p (a c) -> p a c", a=4)
                nc.vector.tensor_scalar(s0, g, 0.0, 2.0, ALU.is_ge, ALU.mult)
                then(nc.vector.scalar_tensor_tensor(out=s1, in0=g, scalar=-1.0, in1=g, op0=ALU.mult, op1=ALU.max))
                nc.vector.tensor_scalar(s0, s0, 1.0, None, ALU.subtract)
                then(nc.vector.tensor_scalar(s1, s1, 0.25, None, ALU.max))
                then(nc.vector.tensor_tensor(g, s0, s1, ALU.mult))
            for b in range(BATCH):
                then(nc.vector.tensor_tensor(wout_g[:, b, :, :], wout_s[:, :, :],
                                             mod[:, 0, b, GA, :].unsqueeze(1).broadcast_to([P, ND, C]), ALU.mult))
            dve.sem_inc(S["scan_done"], 4)
            dve.sem_inc(S["carried"], 2)
            for c in range(NCHUNK):
                b, q = c // 2, c % 2
                if c % 2 == 0:
                    then(nc.vector.memset(carry[:, :, :], 0.0))
                dve.wait_ge(S["dtlow_sb"], c + 1)
                rows = ps[R:R + 2 * NS, BC_BANK, :]
                then(nc.vector.tensor_copy(bc3[0:2 * NS, :], rows))
                then(nc.vector.tensor_tensor(bc_rest[:, :], rows, bc3[0:2 * NS, :], ALU.subtract))
                then(nc.vector.tensor_copy(bc_hi[:, :], bc_rest[:, :]))
                nc.vector.tensor_copy(bc3[2 * NS:4 * NS, :], bc_hi[:, :])
                nc.vector.tensor_tensor(bc3[4 * NS:6 * NS, :], bc_rest[:, :], bc_hi[:, :], ALU.subtract).then_inc(S["bc3_ready"], 1)
                for d in range(ND):
                    dve.wait_ge(S["softp_done"], 2 * c + d + 1)
                    then(nc.vector.tensor_tensor(dtT[:, d, :], dtT[:, d, :], softp[:, d, :], ALU.add))
                    nc.vector.tensor_tensor(uT[:, d, :], dtT[:, d, :], xcT[:, q, d, :], ALU.mult).then_inc(S["dt_ready"], 1)
                def scans(g, n, k):
                    dve.wait_ge(S["bu_ready"], g + 3)
                    dve.wait_ge(S["carried"], g + 1)
                    for d in range(ND):
                        dve.wait_ge(S["a_ready"], g * 2 + (d + 1))
                        nc.vector.tensor_tensor_scan(hs[:, k, d, :], bank(1 + 2 * k + d), bu[:, k, d, :], carry[:, d, bass.ds(n, 1)],
                                                     ALU.mult, ALU.add).then_inc(S["scan_done"], 1)

                def products(g, n, k):
                    dve.wait_ge(S["scan_done"], g * 2 + 6)
                    dve.wait_ge(S["c_ps"], g + 1)
                    dve.wait_ge(S["sum_done"], g + 1)
                    nc.vector.tensor_tensor(prod[:, k, :, :], hs[:, k, :, :], bank(TP).unsqueeze(1).broadcast_to([P, ND, CHUNK]),
                                            ALU.mult).then_inc(S["prod_ready"], 1)
                    nc.vector.tensor_copy(carry[:, :, bass.ds(n, 1)], hs[:, k, :, CHUNK - 1:CHUNK]).then_inc(S["carried"], 1)

                g0 = c * NS
                scans(g0, 0, 0)
                with dve.Fori(0, NS // 2 - 1) as i:
                    for k in range(2):
                        g, n = i * 2 + (g0 + k), i * 2 + k
                        scans(g + 1, n + 1, 1 - k)
                        products(g, n, k)
                scans(g0 + NS - 1, NS - 1, 1)
                products(g0 + NS - 2, NS - 2, 0)
                products(g0 + NS - 1, NS - 1, 1)
                dve.wait_ge(S["sum_done"], c * NS + NS + 2)
                dve.wait_ge(S["zs_ready"], 2 * c + 2)
                if c == 0:
                    dve.wait_ge(S["zeroed"], 16 * (-(-ST0 // 6) + -(-ST1 // 6)))
                nc.vector.tensor_tensor(yT[:, :, :], bank(Y_BANK, 2), zsT[:, q, :, :], ALU.mult).then_inc(S["y_ready"], 1)
                dve.wait_ge(S["o_ps"], c + 1)
                xs = x_tok[:, c * CT:(c + 1) * CT, :]
                nc.vector.tensor_tensor(xs, xs, bank(BC_BANK).rearrange("p (t c) -> p t c", c=C), ALU.add).then_inc(S["x_added"], 1)
                dve.wait_ge(S["x_added"], c + 1)
                norm_rows(1, c)
                take_logits(0, c, E0)
            pick(0, E0, ST0)
            dve.wait_ge(S["in_w1"], 64)
            dve.sem_inc(S["up_sb0"], 2)
            dve.sem_inc(S["dn_sb0"], 2)

            def at(j):
                return slice(j, j + 1) if isinstance(j, int) else bass.ds(j, 1)

            def expert_of(l, j, n):
                return dve.value_load(tile_i[0:1, l, at(j)], min_val=0, max_val=n - 1)

            def bias_up(j, u):
                e = expert_of(0, j, E0)
                dve.wait_ge(S["up_ps0"], j + 3)
                dve.wait_ge(S["ht_ps0"], j + 1)
                nc.vector.tensor_tensor(hp0[:, u, :], bank(2 + u), b1_s[:, bass.ds(e, 1), :].rearrange("p a f -> p (a f)"),
                                        ALU.add).then_inc(S["up_sb0"], 1)

            def bias_down(j, j2, u):
                e = expert_of(0, j, E0)
                dve.wait_ge(S["dn_ps0"], j + 3)
                if j2 is not None:
                    dve.wait_ge(saved[0, u], j2 * 16)
                nc.vector.tensor_tensor(ys0[:, u, :], ps[:, 6 + u, 0:C], b2_s[:, bass.ds(e, 1), :].rearrange("p a c -> p (a c)"),
                                        ALU.add).then_inc(S["dn_sb0"], 1)

            bias_up(0, 0)
            bias_up(1, 1)
            for u in range(2):
                bias_up(u + 2, u)
                bias_down(u, None, u)
            with dve.Fori(0, (ST0 - 4) // 2) as i:
                for u in range(2):
                    bias_up(i * 2 + (u + 4), u)
                    bias_down(i * 2 + (u + 2), i + 1, u)
            for u in range(2):
                bias_down(ST0 - 2 + u, ST0 // 2 - 1, u)
            for c in range(NCHUNK):
                dve.wait_ge(S["gathered0"], 16 * 2 * NTILE)
                ts = slice(c * CT, (c + 1) * CT)
                for t in range(c * CT, (c + 1) * CT):
                    ins = nc.vector.tensor_scalar(y0[0][:, t, :], y0[0][:, t, :], wts[:, 0, t:t + 1], None, ALU.mult)
                then(ins)
                for t in range(c * CT, (c + 1) * CT):
                    ins = nc.vector.scalar_tensor_tensor(out=y0[0][:, t, :], in0=y0[1][:, t, :], scalar=wts[:, 1, t:t + 1],
                                                         in1=y0[0][:, t, :], op0=ALU.mult, op1=ALU.add)
                then(ins)
                then(nc.vector.tensor_tensor(y0[0][:, ts, :], y0[0][:, ts, :], mod[:, 0, c // 2, GB, :].unsqueeze(1).broadcast_to([P, CT, C]), ALU.mult))
                then(nc.vector.tensor_tensor(x_tok[:, ts, :], x_tok[:, ts, :], y0[0][:, ts, :], ALU.add))
                norm_rows(2, c)
                dve.wait_ge(S["rms_sum"], c + 1)
                if c:
                    dve.wait_ge(S["hT_ps"], 2 * NCHUNK + c)
                if c == 0:
                    dve.wait_ge(S["in_l1"], 32)
                    then(nc.vector.tensor_scalar(w4_s[:, :, :], w4_s[:, :, :], vec[:, V["rmsw"]], None, ALU.mult))
                    nc.vector.tensor_tensor(wo_g[:, :, :], mod[:, 1, :, GA, :], wo_s[:, :].unsqueeze(1).broadcast_to([P, BATCH, C]),
                                            ALU.mult).then_inc(S["w_scaled"], 1)
                for t in range(CT):
                    ins = nc.vector.tensor_scalar(xn_tok[:, t, :], h_tok[:, c * CT + t, :], rms_ss[:, c * CT + t:c * CT + t + 1], None, ALU.mult)
                ins.then_inc(S["xn_ready"], 1)
                cs = slice(c * CHUNK, (c + 1) * CHUNK)
                dve.wait_ge(S["p4_side"], c + 1)
                nc.vector.tensor_tensor(bT[:, cs], bank(2), sideT[:, cs], ALU.mult).then_inc(S["b_gated"], 1)
                dve.wait_ge(S["b_gated"], c + 1)
                first = c % 2 == 0
                dve.wait_ge(S["p4_a"], c + 1)
                then(nc.vector.tensor_tensor_scan(scanT[:, cs], aT[:, cs], bT[:, cs], 0.0 if first else scanT[:, c * CHUNK - 1:c * CHUNK],
                                                  ALU.mult, ALU.add))
                dve.wait_ge(S["p4_gate"], c + 1)
                nc.vector.tensor_tensor(gateT[:, cs], gateT[:, cs], scanT[:, cs], ALU.mult).then_inc(S["gated_y"], 1)
            for c in range(NCHUNK):
                ts = slice(c * CT, (c + 1) * CT)
                dve.wait_ge(S["o_ps"], NCHUNK + c + 1)
                dve.wait_ge(S["res_ready"], c + 1)
                then(nc.vector.tensor_tensor(x_tok[:, ts, :], x_tok[:, ts, :], bank(BC_BANK).rearrange("p (t c) -> p t c", c=C), ALU.add))
                nc.vector.tensor_tensor(x_tok[:, ts, :], x_tok[:, ts, :], h_tok[:, ts, :], ALU.add).then_inc(S["x_added"], 1)
                dve.wait_ge(S["x_added"], NCHUNK + c + 1)
                norm_rows(3, c)
                if c == 0:
                    dve.wait_ge(S["in_nw"], 32)
                take_logits(1, c, E1)
            pick(1, E1, ST1)
            dve.wait_ge(S["phase_done"], 1)
            dve.sem_inc(S["up_sb1"], GT)

            def take_up(j, u):
                e = expert_of(1, j, E1)
                js = bass.ds(j, 1)
                dve.wait_ge(S["up_abs1"], j + 1)
                nc.vector.tensor_copy(mag[:, js, :].rearrange("p a h -> p (a h)"), ps[:, 2 + u, 0:H1])
                nc.vector.scalar_tensor_tensor(out=freq[:, js, :].rearrange("p a h -> p (a h)"), in0=ps[:, 2 + u, H1:2 * H1], scalar=0.0,
                                               in1=phase_s[:, bass.ds(e, 1), :].rearrange("p a h -> p (a h)"),
                                               op0=ALU.max, op1=ALU.add).then_inc(S["up_sb1"], 1)

            def turn(g, q):
                gs = bass.ds(g * GT, GT)
                dve.wait_ge(S["theta1"], g + 3)
                dve.wait_ge(S["turned1"], g + 1)
                nc.vector.tensor_scalar(hold[:, q, :, :], freq[:, gs, :], MAGIC, MAGIC, ALU.add, ALU.subtract).then_inc(S["whole1"], 1)
                dve.wait_ge(S["whole1"], g + 1)
                nc.vector.tensor_tensor(freq[:, gs, :], freq[:, gs, :], hold[:, q, :, :], ALU.subtract).then_inc(S["turned1"], 1)

            def take_group(g):
                for k in range(GT):
                    take_up(g * GT + k, k)

            dve.sem_inc(S["turned1"], 1)
            take_group(0)
            take_group(1)
            with dve.Fori(0, NG // 2 - 1) as i:
                for q in range(2):
                    take_group(i * 2 + (q + 2))
                    if True:
                        turn(i * 2 + q, 0)
            turn(NG - 2, 0)
            turn(NG - 1, 0)
            dve.sem_inc(S["ht_sb1"], 2)
            dve.sem_inc(S["dn_sb1"], 2)

            def hidden(j, g, u):
                js = bass.ds(j, 1)
                dve.wait_ge(S["cos1"], g + 1)
                dve.wait_ge(S["ht_ps1"], j + 1)
                nc.vector.tensor_tensor(hd1[:, u, :], mag[:, js, :].rearrange("p a h -> p (a h)"), freq[:, js, :].rearrange("p a h -> p (a h)"),
                                        ALU.mult).then_inc(S["hid1"], 1)

            def copy_ht(j, u):
                dve.wait_ge(S["ht_ps1"], j + 3)
                dve.wait_ge(S["dn_ps1"], j + 1)
                nc.vector.tensor_copy(ht1[:, u, :], ps[:, 4 + u, 0:H1]).then_inc(S["ht_sb1"], 1)

            def copy_y(j, j2, u):
                dve.wait_ge(S["dn_ps1"], j + 3)
                if j2 is not None:
                    dve.wait_ge(saved[1, u], j2 * 16)
                nc.vector.tensor_copy(ys1[:, u, :], ps[:, 6 + u, 0:C]).then_inc(S["dn_sb1"], 1)

            hidden(0, 0, 0)
            hidden(1, 0, 1)
            copy_ht(0, 0)

            def down_steps(j0, g, j2):
                for k in range(GT):
                    hidden(j0 + (k + 2), g + (k + 2) // GT, k % 2)
                    copy_ht(j0 + (k + 1), (k + 1) % 2)
                    before = k // 2 or None if j2 is None else j2 + k // 2
                    copy_y(j0 + k, before, k % 2)

            down_steps(0, 0, None)
            with dve.Fori(0, ST1 // GT - 2) as i:
                down_steps(i * GT + GT, i + 1, i * 2 + 2)
            for j in range(ST1 - GT, ST1):
                if j + 2 < ST1:
                    hidden(j + 2, (j + 2) // GT, j % 2)
                if j + 1 < ST1:
                    copy_ht(j + 1, (j + 1) % 2)
                copy_y(j, j // 2, j % 2)
            for t in range(NTILE):
                dve.wait_ge(S["gathered1"], 16 * 2 * NTILE)
                ins = nc.vector.tensor_scalar(y1[0][:, t, :], y1[0][:, t, :], wts[:, 0, t:t + 1], None, ALU.mult)
            then(ins)
            for t in range(NTILE):
                ins = nc.vector.scalar_tensor_tensor(out=o1[:, t, :], in0=y1[1][:, t, :], scalar=wts[:, 1, t:t + 1], in1=y1[0][:, t, :],
                                                     op0=ALU.mult, op1=ALU.add)
            ins.then_inc(S["o_mix"], 1)
            nc.vector.tensor_tensor(mod[:, 1, :, GB, :], mod[:, 1, :, GB, :], nw_s[:, :].unsqueeze(1).broadcast_to([P, BATCH, C]),
                                    ALU.mult).then_inc(S["dve_chain"], 1)
            chain[0] += 1
            dve.wait_ge(S["o_rstd"], 1)
            dve.wait_ge(S["dve_chain"], chain[0])
            for c in range(NCHUNK):
                ts = slice(c * CT, (c + 1) * CT)
                for t in range(c * CT, (c + 1) * CT):
                    ins = nc.vector.tensor_scalar(o1[:, t, :], o1[:, t, :], ssum[:, t:t + 1], None, ALU.mult)
                then(ins)
                then(nc.vector.tensor_tensor(o1[:, ts, :], o1[:, ts, :], mod[:, 1, c // 2, GB, :].unsqueeze(1).broadcast_to([P, CT, C]), ALU.mult))
                nc.vector.tensor_tensor(x_tok[:, ts, :], x_tok[:, ts, :], o1[:, ts, :], ALU.add).then_inc(S["o_final"], 1)


def kernel(**inputs):
    import numpy as np
    import concourse.bacc as bacc
    from concourse import mybir as _mybir
    from concourse.bass_utils import run_bass_kernel_spmd as run

    w = {k: np.asarray(v) for k, v in inputs.items()}

    def halves(a):
        return a.reshape(ND, P, -1).transpose(1, 0, 2)

    def flat(a):
        return a.reshape(a.shape[0], -1)

    vecs = np.concatenate([
        flat(halves(w["L0_attn_conv_w"])), flat(halves(w["L0_attn_conv_b"])), flat(halves(w["L0_attn_b_dt"])),
        flat(halves(w["L0_attn_A_log"])), flat(halves(w["L0_attn_D_param"])), w["L0_c"].T, w["L1_c"].T,
        w["L1_attn_rms_weight"][:, None], w["L1_attn_b_A"][:, None], w["L0_ffn_router_w"].T, w["L1_ffn_router_w"].T], axis=1)
    consts = np.zeros((P, NCONST), np.float32)
    part, col = np.arange(P)[:, None], np.arange(P)[None, :]
    consts[:, K["ident"]] = part == col
    consts[:, K["tri"]] = part < col
    consts[:, K["sel"]] = part % (2 * NS) == np.arange(2 * NS)[None, :]
    consts[:, K["eiota"]] = np.arange(E1)
    consts[:, K["jiota"]] = np.arange(ST1)
    consts[:, K["reset"]] = np.arange(E1 * NTILE) % NTILE != 0
    arrays = {
        "x": w["L0_attn_x"].reshape(T, C),
        "consts": consts,
        "vecs": vecs,
        "w_in": w["L0_attn_W_in"].T,
        "conv_rows": w["L0_attn_conv_w"].T,
        "w_x": halves(w["L0_attn_W_x"].T),
        "w_dt": w["L0_attn_W_dt"].T,
        "w_out": halves(w["L0_attn_W_out"].T),
        "w1": w["L0_ffn_w1"].transpose(2, 0, 1),
        "b1": w["L0_ffn_b1"],
        "w2": w["L0_ffn_w2"].reshape(E0, C, FK0, P).transpose(3, 0, 2, 1),
        "b2": w["L0_ffn_b2"],
        "wmod": np.stack([w["L0_wmod"], w["L1_wmod"]], axis=1),
        "w4": np.stack([w["L1_attn_w_A"], w["L1_attn_w_x"], w["L1_attn_w_output"], w["L1_attn_w_sidegate"]], axis=1),
        "wo": w["L1_attn_w_o"],
        "mf": np.concatenate([w["L1_ffn_bank_mag"], w["L1_ffn_bank_freq"]], axis=2).transpose(1, 0, 2),
        "phase": w["L1_ffn_bank_phase"],
        "down": w["L1_ffn_bank_down"].reshape(E1, FK1, P, C).transpose(2, 0, 1, 3),
        "norm_w": w["L1_ffn_norm_w"],
        "rbias1": w["L1_ffn_router_bias"],
    }
    nc = bacc.Bacc("TRN2", target_bir_lowering=False, num_devices=1)
    ins, aps = {}, []
    for name, a in arrays.items():
        a = np.ascontiguousarray(a)
        ins[f"in_{name}"] = a
        aps.append(nc.dram_tensor(f"in_{name}", a.shape, _mybir.dt.from_np(a.dtype), kind="ExternalInput").ap())
    out = nc.dram_tensor("out_0", (T, C), F32, kind="ExternalOutput").ap()
    adaln_two_layers(nc, *aps, out)
    r = run(nc, [ins], core_ids=[0])
    return r.results[0]["out_0"].reshape(BATCH, SEQ, C)
```

```python
from contextlib import ExitStack

import concourse.bass as bass
from concourse import mybir

F32 = mybir.dt.float32
BF16 = mybir.dt.bfloat16
I32 = mybir.dt.int32
ALU = mybir.AluOpType
ACT = mybir.ActivationFunctionType
AX = mybir.AxisListType.X

P = 128
BATCH = 2
T = 2048
NTILE = T // P
CHUNK = 512
NCHUNK = T // CHUNK
CT = CHUNK // P
SEQ = T // BATCH
C = 128
DIN = 256
ND = DIN // P
NS = 16
TAPS = 4
PAD = TAPS - 1
R = 64
E0, F0 = 8, 512
E1, H1 = 16, 256
FK0, FK1 = F0 // P, H1 // P
ST0 = (2 * T + E0 * (P - 1)) // P
ST0 += -ST0 % 4
ST1 = (2 * T + E1 * (P - 1)) // P
ST1 += -ST1 % 4
ZT = 4
GT = 4
NG = ST1 // GT
LN_EPS = 1e-5
RMS_EPS1 = 1e-5
RMS_EPS2 = 1e-6
BIG = 64.0
LOWEST = -3.0e38
MAGIC = 1.5 * 2.0 ** 23
TURN = 6.283185
PI = 3.141592653589793
SA, CA, GA, SB, CB, GB = range(6)
TP, C_BANK, Y_BANK = 0, 5, 6
PROJ = ((1, 2, 3, 4), (5, 6, 7, 0))
W0, W1 = 3, 4
STEPS = NCHUNK * NS
BLOAD = 2


def columns(widths):
    at, out = 0, {}
    for name, w in widths:
        out[name] = slice(at, at + w)
        at += w
    return out, at


V, NVEC = columns([("conv", ND * TAPS), ("convb", ND), ("bdt", ND), ("alog", ND * NS), ("dskip", ND),
                   ("c", 2 * BATCH), ("rmsw", 1), ("ba", 1), ("rw0", E0), ("rw1", E1)])
K, NCONST = columns([("ident", P), ("tri", P), ("sel", NS), ("eiota", E1), ("jiota", ST1),
                     ("reset", E1 * NTILE)])


def adaln_two_layers(nc, x, consts, vecs, w_in, conv_rows, w_x, w_dt, w_out, w1, b1, w2, b2, wmod,
                     w4, wo, mf, phase, down, norm_w, rbias1, out):
    slots_in = [nc.dram_tensor(f"slots_in{l}", (n * P, C), F32, kind="Internal").ap()
                for l, n in enumerate((ST0, ST1))]
    slots_out = [nc.dram_tensor(f"slots_out{l}", (n * P, C), F32, kind="Internal").ap()
                 for l, n in enumerate((ST0, ST1))]
    b_rows = nc.dram_tensor("b_rows", (NCHUNK, NS, CHUNK), F32, kind="Internal").ap()
    x_rows = x.rearrange("(t p) c -> p t c", p=P)
    out_rows = out.rearrange("(t p) c -> p t c", p=P)

    ctx = ExitStack()
    with ctx:
        start_at = 16512
        top = [start_at]

        def place(name, shape, dt=F32, at=None):
            size = 2 if dt == BF16 else 4
            for s in shape[1:]:
                size *= s
            begin = top[0] if at is None else at
            end = begin + (size + 31) // 32 * 32
            if at is None:
                top[0] = end
            assert end <= 229344, (name, end)
            return nc.alloc_sbuf_tensor_at(name, shape, dt, offset=begin), end

        def put(name, shape, dt=F32):
            return place(name, shape, dt)[0]

        def sem(name):
            return ctx.enter_context(nc.semaphore(name))

        x_tok = put("x_tok", [P, NTILE, C])
        h_at = top[0]
        h_tok = put("h_tok", [P, NTILE, C])
        hT_at = top[0]
        hT = put("hT", [P, BATCH, PAD + SEQ])
        cst = put("cst", [P, NCONST])
        vec = put("vec", [P, NVEC])
        mod = put("mod", [P, 2, BATCH, 6, C])
        tri_b = put("tri_b", [P, P], BF16)
        ones_b = put("ones_b", [P, P], BF16)
        ones_f = put("ones_f", [P, E1])
        stats = put("stats", [P, CT, 6])
        ln_sum = put("ln_sum", [P, NCHUNK, CT])
        ln_dif = put("ln_dif", [P, NCHUNK, CT])
        ln_m2 = put("ln_m2", [P, NCHUNK, CT])
        ln_mean = put("ln_mean", [P, NCHUNK, CT])
        ln_rs = put("ln_rs", [P, NCHUNK, CT])
        NRT = 9
        route_at = top[0]
        route = put("route", [P, NRT, E1 * NTILE])
        mask_b = put("mask_b", [P, E1 * NTILE], BF16)
        m12 = put("m12", [P, 2, NTILE])
        low = put("low", [P, NTILE])
        ssum = put("ssum", [P, NTILE])
        slot_f = put("slot_f", [P, NTILE])
        slot_i = put("slot_i", [P, 2, NTILE], I32)
        wts = put("wts", [P, 2, NTILE])
        tiles_e = put("tiles_e", [P, 4, E1])
        tile_f = put("tile_f", [P, ST1])
        tile_i = put("tile_i", [P, 2, ST1], I32)
        sc_at = top[0]
        sc_wide = put("sc_wide", [P, 2 * BATCH, P])
        zero_s, _ = place("zero_s", [P, ZT * C], at=sc_at)
        eps_s = put("eps_s", [P, 3])
        neg_a = put("neg_a", [P, ND, NS])
        hR = put("hR", [P, CHUNK])
        nw_s = put("nw_s", [P, C])
        rb1_s = put("rb1_s", [P, E1])
        xcmp_at = top[0]
        xcmp = put("xcmp", [1, ST1 * E1])
        f0_at = top[0]

        w1_s, e = place("w1_s", [P, E0, F0], at=f0_at)
        b1_s, e = place("b1_s", [P, E0, F0], at=e)
        w2_s, e = place("w2_s", [P, E0, FK0, C], at=e)
        b2_s, m_at = place("b2_s", [P, E0, C], at=e)
        aT, e = place("aT", [P, T], at=f0_at)
        bT, e = place("bT", [P, T], at=e)
        sideT, e = place("sideT", [P, T], at=e)
        gateT, e = place("gateT", [P, T], at=e)
        scanT, e = place("scanT", [P, T], at=e)
        w4_s, e = place("w4_s", [P, 4, C], at=e)
        wo_s, e = place("wo_s", [P, C], at=e)
        wo_g, e = place("wo_g", [P, BATCH, C], at=e)
        rms_ss, e = place("rms_ss", [P, NTILE], at=e)
        rms_sq, e = place("rms_sq", [P, CT, C], at=e)
        assert e <= m_at
        freq, e = place("freq", [P, ST1, H1], at=f0_at)
        assert e <= m_at
        y1 = [None, None]
        y1[0], e = place("y1a", [P, NTILE, C], at=f0_at)
        y1[1], e = place("y1b", [P, NTILE, C], at=e)
        o1, e = place("o1", [P, NTILE, C], at=e)
        o1sq, e = place("o1sq", [P, NTILE, C], at=e)
        assert e <= m_at

        win_s, e = place("win_s", [P, 2 * DIN], at=m_at)
        wconv, e = place("wconv", [P, TAPS, DIN], at=e)
        wx_s, e = place("wx_s", [P, ND, R + 2 * NS], at=e)
        wdt_s, e = place("wdt_s", [R, DIN], at=e)
        wout_g, e = place("wout_g", [P, BATCH, ND, C], at=e)
        diag_d, e = place("diag_d", [P, ND, P], at=e)
        sel_b, e = place("sel_b", [3 * 2 * NS, NS, P], BF16, at=e)
        wmod_s, _ = place("wmod_s", [P, 2, 6 * C], at=e)
        xcT, e = place("xcT", [P, 2, ND, CHUNK], at=e)
        zsT, e = place("zsT", [P, 2, ND, CHUNK], at=e)
        bc3, e = place("bc3", [3 * 2 * NS, 2, CHUNK], BF16, at=e)
        dtT, e = place("dtT", [P, 2, ND, CHUNK], at=e)
        uT, e = place("uT", [P, 2, ND, CHUNK], at=e)
        b_sb, e = place("b_sb", [P, 2, BLOAD, CHUNK], at=e)
        bu, e = place("bu", [P, 3, ND, CHUNK], at=e)
        a_sb, e = place("a_sb", [P, ND, CHUNK], at=e)
        hs_at = e
        hs, e = place("hs", [P, 2, ND, CHUNK], at=e)
        convr_s, e1 = place("convr_s", [P, TAPS, DIN], at=hs_at)
        wout_s, _ = place("wout_s", [P, ND, C], at=e1)
        prod, e = place("prod", [P, 3, ND, CHUNK], at=e)
        carry, e = place("carry", [P, ND, NS], at=e)
        yT, e = place("yT", [P, ND, CHUNK], at=e)
        softp, e1 = place("softp", [P, ND, CHUNK], at=route_at + E1 * NTILE * 4)
        bc_f, e1 = place("bc_f", [2 * NS, CHUNK], at=e1)
        bc_rest, e1 = place("bc_rest", [2 * NS, CHUNK], at=e1)
        assert e1 <= route_at + NRT * E1 * NTILE * 4
        dtlow, e1 = place("dtlow", [R, CHUNK], at=xcmp_at)
        bc_hi, e1 = place("bc_hi", [2 * NS, CHUNK], BF16, at=e1)
        assert e1 <= xcmp_at + ST1 * E1 * 4
        m_end = e
        mf_s, e = place("mf_s", [P, E1, 2 * H1], at=m_at)
        phase_s, e = place("phase_s", [P, E1, H1], at=e)
        w_end = e
        down_s, e = place("down_s", [P, E1, FK1, C], at=w_end - E1 * H1 * 4)
        assert e <= w_end
        xl0, e = place("xl0", [P, 2, C], at=w_end)
        xt0, e = place("xt0", [P, 2, P], at=e)
        hp0, e = place("hp0", [P, 2, F0], at=e)
        ht0, e = place("ht0", [P, 2, F0], at=e)
        ys0, e = place("ys0", [P, 2, C], at=e)
        y0 = [None, None]
        y0[0], e = place("y0a", [P, NTILE, C], at=e)
        y0[1], e = place("y0b", [P, NTILE, C], at=e)
        xn_tok = y0[1]
        mag, e = place("mag", [P, ST1, H1], at=w_end)
        xl1, e = place("xl1", [P, 2, C], at=h_at)
        xt1, e = place("xt1", [P, 2, P], at=e)
        hd1, e = place("hd1", [P, 2, H1], at=e)
        ht1, e = place("ht1", [P, 2, H1], at=e)
        ys1, e = place("ys1", [P, GT, C], at=e)
        assert e <= hT_at
        fabs, e = place("fabs", [P, 2, GT, H1], at=hT_at)
        hold = route[:, 0:2 * GT, :].rearrange("p (q a) h -> p q a h", q=2)

        ps = ctx.enter_context(nc.psum_tensor("ps", [P, 8, CHUNK], F32))

        def bank(b, n=1):
            return ps[:, b, :] if n == 1 else ps[:, b:b + n, :]

        def chunk_of(buf, c):
            at = PAD + c % 2 * CHUNK
            return buf[:, c // 2, at:at + CHUNK]

        def decay_of(g, d):
            return bank(1 + d) if g % 2 == 0 else a_sb[:, d, :]

        ident = cst[:, K["ident"]]
        conv_b, b_dt, d_skip = vec[:, V["convb"]], vec[:, V["bdt"]], vec[:, V["dskip"]]

        names = ("in_small in_x in_wmod in_ssm in_w1 in_l1 in_nw in_phase in_down zeros_set zeroed mod_silu mod_ps mod_done "
                 "consts_b ln_stats ln_rstd h_ready hT_ps hT_sb conv_ps z_ps xc_ready zs_ready dbl_ps dtlow_sb "
                 "bc3_ready dt_ps softp_done dt_ready bcf_ready b_rows_saved z_raw c_ps a_ready bu_ready scan_done prod_ready "
                 "sum_done y_ready o_ps x_added logit_ps logit_sb wts_ready neg_ready pad_zeroed "
                 "mask_ready rank_ps pick_exp pick_exp_done slots_ready scattered "
                 "xt_ps0 xt_sb0 up_ps0 up_sb0 ht_ps0 ht_sb0 dn_ps0 dn_sb0 gathered0 "
                 "rms_sum rms_rstd xn_ready p4_ps p4_a p4_side p4_gate gated_y b_gated carried whole1 res_ready in_f1 "
                 "xt_ps1 xt_sb1 up_ps1 up_abs1 up_sb1 soft_e1 soft_l1 theta1 turned1 cos1 tanh1 hid1 ht_ps1 ht_sb1 dn_ps1 dn_sb1 gathered1 "
                 "o_mix o_rstd o_final stored act_chain dve_chain pool_chain phase_done w_scaled").split()
        S = {n: sem(n) for n in names}
        loaded = {(l, u): sem(f"slot_loaded{l}_{u}") for l in range(2) for u in range(2)}
        gathered = {(l, c): sem(f"gathered{l}_{c}") for l in range(2) for c in range(NCHUNK)}
        b_loaded = [sem(f"b_loaded{u}") for u in range(2)]
        YS = (2, GT)
        saved = {(l, u): sem(f"slot_saved{l}_{u}") for l in range(2) for u in range(YS[l])}

        def save(eng, l, n, ys):
            with eng.Fori(0, n // 4) as i:
                for k in range(4):
                    eng.wait_ge(S[f"dn_sb{l}"], i * 4 + (k + 3))
                    eng.dma_start(slots_out[l][bass.ds(i * (4 * P) + k * P, P), :], ys[:, k % YS[l], :]).then_inc(saved[l, k % YS[l]], 16)

        block = ctx.enter_context(nc.Block())

        @block.sync
        def _(sp):
            sp.dma_start(vec[:, :], vecs).then_inc(S["in_small"], 16)
            sp.dma_start(cst[:, :], consts).then_inc(S["in_small"], 16)
            for c in range(NCHUNK):
                sp.dma_start(x_tok[:, c * CT:(c + 1) * CT, :], x_rows[:, c * CT:(c + 1) * CT, :]).then_inc(S["in_x"], 16)
            sp.dma_start(wmod_s[:, :, :], wmod).then_inc(S["in_wmod"], 16)
            for dst, src in ((win_s[:, :], w_in), (convr_s[:, :, :], conv_rows.partition_broadcast(P)),
                             (wx_s[:, :, :], w_x), (wdt_s[:, :], w_dt), (wout_s[:, :, :], w_out)):
                sp.dma_start(dst, src).then_inc(S["in_ssm"], 16)
            later = []
            for e in range(E0):
                es = slice(e, e + 1)
                later += [(w1_s[:, es, :], w1[:, es, :], "in_w1"), (b1_s[:, es, :], b1[es].partition_broadcast(P), "in_w1"),
                          (w2_s[:, es, :, :], w2[:, es, :, :], "in_w1")]
            later += [(b2_s[:, :, :], b2.partition_broadcast(P), "in_w1"), (nw_s[:, :], norm_w.partition_broadcast(P), "in_nw"),
                      (rb1_s[:, :], rbias1.partition_broadcast(P), "in_nw")]
            for l, n in enumerate((ST0, ST1)):
                rows = slots_in[l].rearrange("(p a) c -> p (a c)", p=P)
                for at in range(0, n, ZT):
                    later.append((rows[:, at * C:(at + ZT) * C], zero_s[:, :], "zeroed"))
            sp.wait_ge(S["zeros_set"], 1)
            for c in range(NCHUNK):
                sp.wait_ge(S["bcf_ready"], c + 1)
                sp.dma_start(b_rows[c], bc_f[0:NS, :]).then_inc(S["b_rows_saved"], 16)
                sp.wait_ge(S["b_rows_saved"], 16 * (c + 1))
                for k in range(c * NS // BLOAD, (c + 1) * NS // BLOAD):
                    if k >= 2:
                        sp.wait_ge(S["bu_ready"], BLOAD * (k - 1))
                    n = k * BLOAD - c * NS
                    sp.dma_start(b_sb[:, k % 2, :, :], b_rows[c, n:n + BLOAD, :].partition_broadcast(P)).then_inc(b_loaded[k % 2], 16)
                    for dst, src, done in later[2 * k - 8:2 * k - 6] if k >= 4 else ():
                        sp.dma_start(dst, src).then_inc(S[done], 16)
            sp.wait_ge(S["x_added"], NCHUNK)
            sp.dma_start(mf_s[:, :, :], mf).then_inc(S["in_f1"], 16)
            sp.dma_start(phase_s[:, :, :], phase.partition_broadcast(P)).then_inc(S["in_phase"], 16)

            def slot_loads(l, n, xl):
                sp.wait_ge(S["scattered"], 16 * 2 * NTILE * (l + 1))
                with sp.Fori(0, n // 4) as i:
                    for k in range(4):
                        sp.wait_ge(S[f"xt_ps{l}"], i * 4 + (k + 1))
                        sp.dma_start(xl[:, k % 2, :], slots_in[l][bass.ds(i * (4 * P) + k * P, P), :]).then_inc(loaded[l, k % 2], 16)

            sp.sem_inc(S["xt_ps0"], 2)
            slot_loads(0, ST0, xl0)
            sp.wait_ge(S["dn_sb0"], ST0 + 2)
            sp.dma_start(w4_s[:, :, :], w4).then_inc(S["in_l1"], 16)
            sp.dma_start(wo_s[:, :], wo).then_inc(S["in_l1"], 16)
            sp.sem_inc(S["xt_ps1"], 2)
            slot_loads(1, ST1, xl1)
            sp.wait_ge(S["up_sb1"], ST1 + GT)
            sp.dma_start(down_s[:, :, :, :], down).then_inc(S["in_down"], 16)
            save(sp, 1, ST1, ys1)
            for c in range(NCHUNK):
                sp.wait_ge(S["o_final"], c + 1)
                sp.dma_start(out_rows[:, c * CT:(c + 1) * CT, :], x_tok[:, c * CT:(c + 1) * CT, :]).then_inc(S["stored"], 16)
            sp.wait_ge(S["stored"], 16 * NCHUNK)

        @block.gpsimd
        def _(pool):
            def scatter(l):
                pool.wait_ge(S["slots_ready"], l + 1)
                pool.wait_ge(S["zeroed"], 16 * (ST0 + ST1) // ZT)
                for t in range(NTILE):
                    for k in range(2):
                        pool.indirect_dma_start(slots_in[l], bass.IndirectOffsetOnAxis(ap=slot_i[:, k, t:t + 1], axis=0),
                                                h_tok[:, t, :], None).then_inc(S["scattered"], 16)

            def gather(l, n, y):
                for u in range(YS[l]):
                    pool.wait_ge(saved[l, u], 16 * (n // YS[l]))
                for t in range(NTILE):
                    for k in range(2):
                        pool.indirect_dma_start(y[k][:, t, :], None, slots_out[l],
                                                bass.IndirectOffsetOnAxis(ap=slot_i[:, k, t:t + 1], axis=0)
                                                ).then_inc(gathered[l, t // CT], 16)


            pool.memset(ones_b[:, :], 1.0).then_inc(S["consts_b"], 1)
            pool.memset(ones_f[:, :], 1.0).then_inc(S["consts_b"], 1)
            pool.memset(eps_s[:, 0:1], LN_EPS).then_inc(S["consts_b"], 1)
            pool.memset(eps_s[:, 1:2], RMS_EPS2).then_inc(S["consts_b"], 1)
            pool.memset(eps_s[:, 2:3], (0.1 + PI / 2) / (2 * PI)).then_inc(S["consts_b"], 1)
            pool.wait_ge(S["mod_ps"], 2 * BATCH)
            pool.memset(zero_s[:, :], 0.0).then_inc(S["zeros_set"], 1)
            pool.memset(hT[:, :, 0:PAD], 0.0).then_inc(S["pad_zeroed"], 1)
            for g in range(STEPS):
                c, n = divmod(g, NS)
                if n == 0:
                    pool.wait_ge(S["dt_ready"], 2 * c + 2)
                pool.wait_ge(b_loaded[g // BLOAD % 2], 16 * (g // BLOAD // 2 + 1))
                if g >= 3:
                    pool.wait_ge(S["scan_done"], 2 * (g - 2))
                nc.gpsimd.tensor_tensor(bu[:, g % 3, :, :], uT[:, c % 2, :, :],
                                        b_sb[:, g // BLOAD % 2, g % BLOAD, :].unsqueeze(1).broadcast_to([P, ND, CHUNK]),
                                        ALU.mult).then_inc(S["bu_ready"], 1)
            scatter(0)
            save(pool, 0, ST0, ys0)
            gather(0, ST0, y0)
            for c in range(NCHUNK):
                ts = slice(c * CT, (c + 1) * CT)
                pool.wait_ge(S["xn_ready"], c + 1)
                pool.wait_ge(S["rms_sum"], c + 1)
                ga = mod[:, 1, c // 2, GA, :].unsqueeze(1).broadcast_to([P, CT, C])
                nc.gpsimd.tensor_tensor(h_tok[:, ts, :], h_tok[:, ts, :], ga, ALU.mult).then_inc(S["res_ready"], 1)
            scatter(1)
            for g in range(NG):
                gs = slice(g * GT, (g + 1) * GT)
                pool.wait_ge(S["whole1"], g + 1)
                nc.gpsimd.tensor_tensor(freq[:, gs, :], freq[:, gs, :], hold[:, g % 2, :, :], ALU.subtract).then_inc(S["turned1"], 1)
            gather(1, ST1, y1)

        @block.scalar
        def _(act):
            chain = [0]

            def then(ins):
                chain[0] += 1
                ins.then_inc(S["act_chain"], 1)
                act.wait_ge(S["act_chain"], chain[0])

            LOG_EXP, SILU_TANH_SIN, SIGMOID = "natural_log_exp_and_others", "silu_and_others", "sigmoid_and_others"

            def rstd(s, c):
                act.wait_ge(S["ln_stats"], s * NCHUNK + c + 1)
                then(nc.scalar.activation(ln_rs[:, c, :], ln_m2[:, c, :], ACT.Ln, bias=vec_eps(LN_EPS), scale=1.0 / C))
                nc.scalar.activation(ln_rs[:, c, :], ln_rs[:, c, :], ACT.Exp, scale=-0.5).then_inc(S["ln_rstd"], 1)

            def vec_eps(v):
                return eps_s[:, {LN_EPS: 0, RMS_EPS2: 1}[v]:{LN_EPS: 0, RMS_EPS2: 1}[v] + 1]

            act.wait_ge(S["in_small"], 32)
            act.wait_ge(S["consts_b"], 5)
            nc.scalar.activation(sc_wide[:, :, :], vec[:, V["c"]].unsqueeze(2).broadcast_to([P, 2 * BATCH, P]), ACT.Silu).then_inc(S["mod_silu"], 1)
            nc.scalar.activation(neg_a[:, :, :], vec[:, V["alog"]].rearrange("p (d n) -> p d n", d=ND), ACT.Exp).then_inc(S["neg_ready"], 1)
            act.preload_act_table_set(LOG_EXP)
            for c in range(NCHUNK):
                rstd(0, c)

            def columns_first(c):
                act.wait_ge(S["hT_ps"], c + 1)
                act.wait_ge(S["pad_zeroed"], 1)
                nc.scalar.activation(chunk_of(hT, c), bank(TP), ACT.Copy).then_inc(S["hT_sb"], 1)

            def z_copy(c):
                if c >= 2:
                    act.wait_ge(S["y_ready"], c - 1)
                for d in range(ND):
                    act.wait_ge(S["z_ps"], 2 * c + d + 1)
                    nc.scalar.activation(zsT[:, c % 2, d, :], bank(W0 + d), ACT.Copy).then_inc(S["z_raw"], 1)

            def silus(c):
                act.preload_act_table_set(SILU_TANH_SIN)
                for d in range(ND):
                    act.wait_ge(S["conv_ps"], 2 * c + d + 1)
                    nc.scalar.activation(xcT[:, c % 2, d, :], bank(W1 - d), ACT.Silu, bias=conv_b[:, d:d + 1]).then_inc(S["xc_ready"], 1)
                act.wait_ge(S["z_raw"], 2 * c + 2)
                for d in range(ND):
                    nc.scalar.activation(zsT[:, c % 2, d, :], zsT[:, c % 2, d, :], ACT.Silu).then_inc(S["zs_ready"], 1)
                act.preload_act_table_set(LOG_EXP)

            def low_and_rows(c):
                act.wait_ge(S["dbl_ps"], c + 1)
                if c:
                    act.wait_ge(S["bc3_ready"], c)
                    act.wait_ge(S["b_rows_saved"], 16 * c)
                nc.scalar.activation(dtlow[:, :], ps[0:R, W1, :], ACT.Copy).then_inc(S["dtlow_sb"], 1)
                nc.scalar.activation(bc_f[:, :], ps[R:R + 2 * NS, W1, :], ACT.Copy).then_inc(S["bcf_ready"], 1)

            def softplus(c, d):
                act.wait_ge(S["dt_ps"], 2 * c + d + 1)
                if c:
                    act.wait_ge(S["dt_ready"], 2 * c)
                nc.scalar.activation(dtT[:, c % 2, d, :], bank(W0 + d), ACT.Relu, bias=b_dt[:, d:d + 1])
                then(nc.scalar.activation(softp[:, d, :], bank(W0 + d), ACT.Abs, bias=b_dt[:, d:d + 1]))
                then(nc.scalar.activation(softp[:, d, :], softp[:, d, :], ACT.Exp, scale=-1.0))
                nc.scalar.activation(softp[:, d, :], softp[:, d, :], ACT.Ln, bias=1.0).then_inc(S["softp_done"], 1)

            def decays(g):
                c, n = divmod(g, NS)
                if n == 0:
                    act.wait_ge(S["dt_ready"], 2 * c + 2)
                for d in range(ND):
                    if g >= 2:
                        act.wait_ge(S["scan_done"], 2 * (g - 2) + d + 1)
                    nc.scalar.activation(decay_of(g, d), dtT[:, c % 2, d, :], ACT.Exp,
                                         scale=neg_a[:, d, n:n + 1]).then_inc(S["a_ready"], 1)

            def columns_out(c):
                act.wait_ge(S["hT_ps"], NCHUNK + c + 1)
                if c:
                    act.wait_ge(S["logit_ps"], c)
                nc.scalar.activation(hR[:, :], bank(W0), ACT.Copy).then_inc(S["hT_sb"], 1)

            before = {2: z_copy, 8: silus, 9: low_and_rows, 10: lambda c: softplus(c, 0), 11: lambda c: softplus(c, 1)}
            after = {6: lambda c: rstd(1, c), 12: columns_out}
            columns_first(0)
            z_copy(0)
            silus(0)
            columns_first(1)
            low_and_rows(0)
            columns_first(2)
            softplus(0, 0)
            softplus(0, 1)
            columns_first(3)
            act.wait_ge(S["neg_ready"], 2)
            decays(0)
            decays(1)
            for g in range(STEPS):
                c, n = divmod(g, NS)
                if g + 2 < STEPS:
                    decays(g + 2)
                if n in before and c + 1 < NCHUNK:
                    before[n](c + 1)
                if n in after and c:
                    after[n](c - 1)
            for n in sorted(after):
                after[n](NCHUNK - 1)
            act.wait_ge(S["pick_exp"], 1)
            nc.scalar.activation(route[:, 8, 0:E0 * NTILE], route[:, 8, 0:E0 * NTILE], ACT.Exp).then_inc(S["pick_exp_done"], 1)
            act.sem_inc(S["xt_sb0"], 2)
            act.sem_inc(S["ht_sb0"], 2)

            def copy_xt(l, xt, j, u):
                act.wait_ge(S[f"xt_ps{l}"], j + 3)
                nc.scalar.activation(xt[:, u, :], ps[:, u, 0:P], ACT.Copy).then_inc(S[f"xt_sb{l}"], 1)

            def relu_ht(j, u):
                act.wait_ge(S["ht_ps0"], j + 3)
                nc.scalar.activation(ht0[:, u, :], bank(4 + u), ACT.Relu).then_inc(S["ht_sb0"], 1)

            copy_xt(0, xt0, 0, 0)
            copy_xt(0, xt0, 1, 1)
            with act.Fori(0, (ST0 - 4) // 4) as i:
                for k in range(4):
                    copy_xt(0, xt0, i * 4 + (k + 2), k % 2)
                    relu_ht(i * 4 + k, k % 2)
            for j in range(ST0 - 4, ST0):
                if j + 2 < ST0:
                    copy_xt(0, xt0, j + 2, j % 2)
                relu_ht(j, j % 2)
            def rms_rows(c):
                act.wait_ge(S["h_ready"], 2 * NCHUNK + c + 1)
                for t in range(c * CT, (c + 1) * CT):
                    ins = nc.scalar.activation(rms_sq[:, t % CT, :], h_tok[:, t, :], ACT.Square, accum_out=rms_ss[:, t:t + 1])
                then(ins)
                ss = rms_ss[:, c * CT:(c + 1) * CT]
                then(nc.scalar.activation(ss, ss, ACT.Ln, bias=vec_eps(RMS_EPS1), scale=1.0 / C))
                nc.scalar.activation(ss, ss, ACT.Exp, scale=-0.5).then_inc(S["rms_sum"], 1)

            def columns_in(c):
                act.wait_ge(S["hT_ps"], 2 * NCHUNK + c + 1)
                nc.scalar.activation(chunk_of(hT, c), bank(TP), ACT.Copy).then_inc(S["hT_sb"], 1)

            def sigmoids(c):
                cs = slice(c * CHUNK, (c + 1) * CHUNK)
                banks = PROJ[c % 2]
                act.wait_ge(S["p4_ps"], 4 * c + 1)
                nc.scalar.activation(aT[:, cs], bank(banks[0]), ACT.Sigmoid, bias=vec[:, V["ba"]]).then_inc(S["p4_a"], 1)
                act.wait_ge(S["p4_ps"], 4 * c + 3)
                nc.scalar.activation(sideT[:, cs], bank(banks[2]), ACT.Sigmoid).then_inc(S["p4_side"], 1)
                act.wait_ge(S["p4_ps"], 4 * c + 4)
                nc.scalar.activation(gateT[:, cs], bank(banks[3]), ACT.Sigmoid).then_inc(S["p4_gate"], 1)

            def columns_router(c):
                act.wait_ge(S["hT_ps"], 3 * NCHUNK + c + 1)
                nc.scalar.activation(chunk_of(hT, c), bank(PROJ[c % 2][0]), ACT.Copy).then_inc(S["hT_sb"], 1)

            act.preload_act_table_set(LOG_EXP)
            for c in range(NCHUNK + 2):
                if c < NCHUNK:
                    rstd(2, c)
                if 0 < c <= NCHUNK:
                    rms_rows(c - 1)
                if c > 1:
                    columns_in(c - 2)
            act.wait_ge(S["in_f1"], 16)
            act.wait_ge(S["in_phase"], 16)
            nc.scalar.activation(mf_s[:, :, H1:2 * H1], mf_s[:, :, H1:2 * H1], ACT.Copy, scale=1.0 / (2 * PI)).then_inc(S["phase_done"], 1)
            nc.scalar.activation(phase_s[:, :, :], phase_s[:, :, :], ACT.Identity, bias=eps_s[:, 2:3], scale=1.0 / (2 * PI)).then_inc(S["phase_done"], 1)
            act.preload_act_table_set(SIGMOID)
            for c in range(NCHUNK):
                sigmoids(c)
            act.preload_act_table_set(LOG_EXP)
            for c in range(NCHUNK + 2):
                if c < NCHUNK:
                    rstd(3, c)
                if c > 1:
                    columns_router(c - 2)
            act.wait_ge(S["pick_exp"], 2)
            nc.scalar.activation(route[:, 8, 0:NTILE], route[:, 8, 0:NTILE], ACT.Exp).then_inc(S["pick_exp_done"], 1)

            act.sem_inc(S["xt_sb1"], 2)
            act.sem_inc(S["theta1"], 2)
            copy_xt(1, xt1, 0, 0)

            def soft_exp(g, q):
                act.wait_ge(S["up_abs1"], g * GT + GT)
                nc.scalar.activation(fabs[:, q, :, :], fabs[:, q, :, :], ACT.Exp, scale=-2 * PI).then_inc(S["soft_e1"], 1)

            def soft_log(g, q):
                act.wait_ge(S["soft_e1"], g + 1)
                nc.scalar.activation(fabs[:, q, :, :], fabs[:, q, :, :], ACT.Ln, bias=1.0).then_inc(S["soft_l1"], 1)

            def group_abs(g, q, last=False, g1=None):
                act.wait_ge(S["theta1"], g + 1)
                for k in range(GT):
                    j = g * GT + k
                    if not (last and k == GT - 1):
                        copy_xt(1, xt1, j + 1, (k + 1) % 2)
                    act.wait_ge(S["up_ps1"], j + 3)
                    nc.scalar.activation(fabs[:, q, k, :], ps[:, 2 + k, H1:2 * H1], ACT.Abs).then_inc(S["up_abs1"], 1)
                    if g1 is not None:
                        if k == 0:
                            soft_exp(g1, 1 - q)
                        if k == 1:
                            soft_log(g1, 1 - q)

            group_abs(0, 0)
            with act.Fori(0, NG // 2 - 1) as i:
                for q in range(2):
                    group_abs(i * 2 + (q + 1), 1 - q, g1=i * 2 + q)
            group_abs(NG - 1, 1, last=True, g1=NG - 2)
            soft_exp(NG - 1, 1)
            soft_log(NG - 1, 1)
            act.preload_act_table_set(SILU_TANH_SIN)
            act.wait_ge(S["turned1"], NG + 2)
            with act.Fori(0, NG) as g:
                gs = bass.ds(g * GT, GT)
                nc.scalar.activation(mag[:, gs, :], mag[:, gs, :], ACT.Tanh).then_inc(S["tanh1"], 1)
                nc.scalar.activation(freq[:, gs, :], freq[:, gs, :], ACT.Sin, scale=TURN).then_inc(S["cos1"], 1)
            act.preload_act_table_set(LOG_EXP)
            for c in range(NCHUNK):
                act.wait_ge(S["o_mix"], c + 1)
                for t in range(c * CT, (c + 1) * CT):
                    ins = nc.scalar.activation(o1sq[:, t, :], o1[:, t, :], ACT.Square, accum_out=ssum[:, t:t + 1])
                then(ins)
                ss = ssum[:, c * CT:(c + 1) * CT]
                then(nc.scalar.activation(ss, ss, ACT.Ln, bias=vec_eps(RMS_EPS2), scale=1.0 / C))
                nc.scalar.activation(ss, ss, ACT.Exp, scale=-0.5).then_inc(S["o_rstd"], 1)

        @block.tensor
        def _(pe):
            def transposes(s, c, b=TP):
                src = xn_tok if s == 2 else h_tok
                pe.wait_ge(S["xn_ready"] if s == 2 else S["h_ready"], c + 1 if s == 2 else s * NCHUNK + c + 1)
                if s < 3 and (c or s):
                    pe.wait_ge(S["hT_sb"], s * NCHUNK + c)
                for t in range(CT):
                    last = nc.tensor.transpose(ps[:, b, t * P:(t + 1) * P], src[:, c * CT + t, :], ident)
                last.then_inc(S["hT_ps"], 1)

            def logits(l, c, e, b):
                pe.wait_ge(S["hT_sb"], (2 * l + 1) * NCHUNK + c + 1)
                src = hR if l == 0 else chunk_of(hT, c)
                for t in range(CT):
                    last = nc.tensor.matmul(ps[:, b, t * E1:t * E1 + e], src[:, t * P:(t + 1) * P],
                                            vec[:, V[f"rw{l}"]], start=True, stop=True)
                last.then_inc(S["logit_ps"], 1)

            def ranks(l, e):
                pe.wait_ge(S["mask_ready"], l + 1)
                n = e * NTILE
                nc.tensor.matmul(ps[:, 1, 0:n], tri_b[:, :], mask_b[:, 0:n], start=True, stop=True)
                nc.tensor.matmul(ps[:, 2, 0:n], ones_b[:, :], mask_b[:, 0:n], start=True, stop=True).then_inc(S["rank_ps"], 1)

            pe.wait_ge(S["mod_silu"], 1)
            pe.wait_ge(S["in_wmod"], 16)
            pe.wait_ge(S["in_small"], 32)
            for lb, (q0, q1) in enumerate(((1, 2), (3, 4), (5, 6), (7, 0))):
                w = wmod_s[:, lb // BATCH, :]
                nc.tensor.matmul(bank(q0), sc_wide[:, lb, :], w[:, 0:CHUNK], start=True, stop=True)
                nc.tensor.matmul(ps[:, q1, 0:2 * C], sc_wide[:, lb, :], w[:, CHUNK:6 * C], start=True, stop=True).then_inc(S["mod_ps"], 1)
            pe.wait_ge(S["mod_done"], 1)
            def z_half(c, d):
                pe.wait_ge(S["hT_sb"], c + 1)
                if c:
                    pe.wait_ge(S["softp_done"], 2 * c)
                if c >= 3:
                    pe.wait_ge(S["hT_sb"], NCHUNK + c - 2)
                    pe.wait_ge(S["logit_sb"], c - 2)
                b, lo = c // 2, c % 2 * CHUNK + PAD
                nc.tensor.matmul(bank(W0 + d), win_s[:, DIN + d * P:DIN + (d + 1) * P], hT[:, b, lo:lo + CHUNK],
                                 start=True, stop=True).then_inc(S["z_ps"], 1)

            def conv_taps(c, d, k0):
                pe.wait_ge(S["z_raw"], 2 * c + 2)
                if d == 1 and c >= 2:
                    pe.wait_ge(S["x_added"], c - 1)
                pe.wait_ge(S["w_scaled"], 1)
                b, lo = c // 2, c % 2 * CHUNK
                for k in range(k0, k0 + TAPS // 2):
                    last = nc.tensor.matmul(bank(W1 - d), wconv[:, k, d * P:(d + 1) * P], hT[:, b, lo + k:lo + k + CHUNK],
                                            start=k == 0, stop=k == TAPS - 1)
                if k == TAPS - 1:
                    last.then_inc(S["conv_ps"], 1)

            def low_rows(c):
                pe.wait_ge(S["xc_ready"], 2 * c + 2)
                for d in range(ND):
                    last = nc.tensor.matmul(ps[0:R + 2 * NS, W1, :], wx_s[:, d, :], xcT[:, c % 2, d, :], start=d == 0, stop=d == ND - 1)
                last.then_inc(S["dbl_ps"], 1)

            def dt_rows(c):
                pe.wait_ge(S["dtlow_sb"], c + 1)
                pe.wait_ge(S["bcf_ready"], c + 1)
                for d in range(ND):
                    nc.tensor.matmul(bank(W0 + d), wdt_s[:, d * P:(d + 1) * P], dtlow[:, :], start=True, stop=True).then_inc(S["dt_ps"], 1)

            def c_row(g):
                c, n = divmod(g, NS)
                if n == 0:
                    pe.wait_ge(S["bc3_ready"], c + 1)
                nc.tensor.matmul(bank(C_BANK if g % 2 else TP), sel_b[:, n, :], bc3[:, c % 2, :], start=True, stop=True).then_inc(S["c_ps"], 1)

            def skip(c, d):
                nc.tensor.matmul(bank(Y_BANK + d), diag_d[:, d, :], xcT[:, c % 2, d, :], start=False, stop=False)

            def project_out(c):
                if c:
                    pe.wait_ge(S["hT_sb"], NCHUNK + c)
                if c + 2 < NCHUNK:
                    pe.wait_ge(S["z_raw"], 2 * (c + 2) + 1)
                pe.wait_ge(S["y_ready"], c + 1)
                for t in range(CT):
                    for d in range(ND):
                        last = nc.tensor.matmul(ps[:, W0, t * P:(t + 1) * P], yT[:, d, t * P:(t + 1) * P],
                                                wout_g[:, c // 2, d, :], start=d == 0, stop=d == ND - 1)
                last.then_inc(S["o_ps"], 1)

            def rows_back(c):
                if c + 2 < NCHUNK:
                    pe.wait_ge(S["softp_done"], 2 * (c + 2) + 1)
                transposes(1, c, W0)

            def score(c):
                if c + 2 < NCHUNK:
                    pe.wait_ge(S["softp_done"], 2 * (c + 2) + 2)
                if c:
                    pe.wait_ge(S["logit_sb"], c)
                logits(0, c, E0, W1)

            before = {0: lambda c: z_half(c, 0), 1: lambda c: z_half(c, 1),
                      3: lambda c: conv_taps(c, 0, 0), 4: lambda c: conv_taps(c, 0, 2),
                      5: lambda c: conv_taps(c, 1, 0), 6: lambda c: conv_taps(c, 1, 2), 9: low_rows, 10: dt_rows}
            after = {2: project_out, 11: rows_back, 13: score}
            transposes(0, 0)
            pe.wait_ge(S["in_ssm"], 80)
            for n in (0, 1, 3, 4, 5, 6):
                before[n](0)
            transposes(0, 1)
            low_rows(0)
            transposes(0, 2)
            dt_rows(0)
            transposes(0, 3)
            pe.wait_ge(S["hT_sb"], NCHUNK)
            c_row(0)
            c_row(1)
            for g in range(STEPS):
                c, n = divmod(g, NS)
                pe.wait_ge(S["prod_ready"], g + 1)
                if g + 2 < STEPS:
                    c_row(g + 2)
                if n == 0 and c:
                    pe.wait_ge(S["y_ready"], c)
                for d in range(ND):
                    last = nc.tensor.matmul(bank(Y_BANK + d), ident, prod[:, g % 3, d, :], start=n == 0, stop=n == NS - 1)
                last.then_inc(S["sum_done"], 1)
                if n in before and c + 1 < NCHUNK:
                    before[n](c + 1)
                if n in after and c:
                    after[n](c - 1)
                if n in (12, 14):
                    skip(c, n // 14)
            for n in sorted(after):
                after[n](NCHUNK - 1)
            ranks(0, E0)


            def at(j):
                return slice(j, j + 1) if isinstance(j, int) else bass.ds(j, 1)

            def expert_of(l, j, n):
                return pe.value_load(tile_i[0:1, l, at(j)], min_val=0, max_val=n - 1)

            def turn_x(l, xl, j, j2, u):
                pe.wait_ge(loaded[l, u], j2 * 16 + 16)
                nc.tensor.transpose(ps[:, u, 0:P], xl[:, u, :], ident).then_inc(S[f"xt_ps{l}"], 1)

            def up0(j, u):
                e = expert_of(0, j, E0)
                pe.wait_ge(S["xt_sb0"], j + 3)
                nc.tensor.matmul(bank(2 + u), xt0[:, u, :], w1_s[:, bass.ds(e, 1), :].rearrange("p a f -> p (a f)"),
                                 start=True, stop=True).then_inc(S["up_ps0"], 1)

            def turn_h0(j, u):
                pe.wait_ge(S["up_sb0"], j + 3)
                for k in range(FK0):
                    last = nc.tensor.transpose(ps[:, 4 + u, k * P:(k + 1) * P], hp0[:, u, k * P:(k + 1) * P], ident)
                last.then_inc(S["ht_ps0"], 1)

            def down_rows(l, j, u, n, fk, ht, w, e_n):
                e = expert_of(l, j, e_n)
                pe.wait_ge(S[f"ht_sb{l}"], j + 3)
                pe.wait_ge(S[f"dn_sb{l}"], j + 1)
                for k in range(fk):
                    last = nc.tensor.matmul(ps[:, 6 + u, 0:C], ht[:, u, k * P:(k + 1) * P],
                                            w[:, bass.ds(e, 1), k, :].rearrange("p a c -> p (a c)"), start=k == 0, stop=k == fk - 1)
                last.then_inc(S[f"dn_ps{l}"], 1)

            def down0(j, u):
                down_rows(0, j, u, ST0, FK0, ht0, w2_s, E0)

            pe.wait_ge(S["slots_ready"], 1)
            pe.wait_ge(S["in_w1"], 16 * (3 * E0 + 1))
            pe.sem_inc(S["up_ps0"], 2)
            pe.sem_inc(S["ht_ps0"], 2)
            pe.sem_inc(S["dn_ps0"], 2)
            turn_x(0, xl0, 0, 0, 0)
            turn_x(0, xl0, 1, 0, 1)
            up0(0, 0)
            turn_x(0, xl0, 2, 1, 0)
            up0(1, 1)
            turn_h0(0, 0)
            with pe.Fori(0, (ST0 - 4) // 12) as i:
                for k in range(12):
                    j, u = i * 12 + (k + 2), k % 2
                    turn_x(0, xl0, j + 1, i * 6 + (1 + (1 + k) // 2), 1 - u)
                    up0(j, u)
                    turn_h0(j - 1, 1 - u)
                    down0(j - 2, u)
            n = ST0
            turn_x(0, xl0, n - 1, n // 2 - 1, 1)
            up0(n - 2, 0)
            turn_h0(n - 3, 1)
            down0(n - 4, 0)
            up0(n - 1, 1)
            turn_h0(n - 2, 0)
            down0(n - 3, 1)
            turn_h0(n - 1, 1)
            down0(n - 2, 0)
            down0(n - 1, 1)
            pe.wait_ge(S["w_scaled"], 2)
            def project_in(c):
                pe.wait_ge(S["hT_sb"], 2 * NCHUNK + (NCHUNK if c % 2 else c + 1))
                if c >= 2:
                    pe.wait_ge(S["p4_gate"], c - 1)
                    pe.wait_ge(S["x_added"], NCHUNK + c - 1)
                for m, b in enumerate(PROJ[c % 2]):
                    nc.tensor.matmul(bank(b), w4_s[:, m, :], chunk_of(hT, c), start=True, stop=True).then_inc(S["p4_ps"], 1)

            def project_back(c):
                pe.wait_ge(S["gated_y"], c + 1)
                for t in range(CT):
                    last = nc.tensor.matmul(ps[:, PROJ[c % 2][1], t * P:(t + 1) * P], gateT[:, c * CHUNK + t * P:c * CHUNK + (t + 1) * P],
                                            wo_g[:, c // 2, :], start=True, stop=True)
                last.then_inc(S["o_ps"], 1)

            def score_rows(c):
                a, b = PROJ[c % 2][0:2]
                if c < 2:
                    pe.wait_ge(S["p4_a"], c + 3)
                    pe.wait_ge(S["x_added"], NCHUNK + c + 3)
                else:
                    pe.wait_ge(S["hT_sb"], 3 * NCHUNK + c - 1)
                    pe.wait_ge(S["logit_sb"], NCHUNK + c - 1)
                transposes(3, c, a)
                logits(1, c, E1, b)

            for c in range(NCHUNK):
                transposes(2, c)
            for c in range(NCHUNK + 1):
                if c < NCHUNK:
                    project_in(c)
                if c:
                    project_back(c - 1)
            for c in range(NCHUNK):
                score_rows(c)
            ranks(1, E1)
            pe.wait_ge(S["slots_ready"], 2)
            pe.wait_ge(S["phase_done"], 2)

            def up1(j, u):
                e = expert_of(1, j, E1)
                pe.wait_ge(S["xt_sb1"], j + 3)
                pe.wait_ge(S["up_sb1"], j + 1)
                nc.tensor.matmul(bank(2 + u), xt1[:, u % 2, :], mf_s[:, bass.ds(e, 1), :].rearrange("p a f -> p (a f)"),
                                 start=True, stop=True).then_inc(S["up_ps1"], 1)

            pe.sem_inc(S["up_ps1"], 2)
            turn_x(1, xl1, 0, 0, 0)
            with pe.Fori(0, NG // 2 - 1) as i:
                for k in range(2 * GT):
                    j = i * (2 * GT) + k
                    turn_x(1, xl1, j + 1, i * GT + (1 + k) // 2, 1 - k % 2)
                    up1(j, k % GT)
            for j in range(ST1 - 2 * GT, ST1):
                if j + 1 < ST1:
                    turn_x(1, xl1, j + 1, (j + 1) // 2, 1 - j % 2)
                up1(j, j % GT)

            def turn_h1(j, u):
                pe.wait_ge(S["hid1"], j + 1)
                for k in range(FK1):
                    last = nc.tensor.transpose(ps[:, 4 + u, k * P:(k + 1) * P], hd1[:, u, k * P:(k + 1) * P], ident)
                last.then_inc(S["ht_ps1"], 1)

            def down1(j, u):
                down_rows(1, j, u, ST1, FK1, ht1, down_s, E1)

            pe.sem_inc(S["ht_ps1"], 2)
            pe.sem_inc(S["dn_ps1"], 2)
            turn_h1(0, 0)
            pe.wait_ge(S["in_down"], 16)
            with pe.Fori(0, NG // 2 - 1) as i:
                for k in range(2 * GT):
                    turn_h1(i * (2 * GT) + (k + 1), 1 - k % 2)
                    down1(i * (2 * GT) + k, k % 2)
            for j in range(ST1 - 2 * GT, ST1):
                if j + 1 < ST1:
                    turn_h1(j + 1, 1 - j % 2)
                down1(j, j % 2)

        @block.vector
        def _(dve):
            chain = [0]

            def then(ins):
                chain[0] += 1
                ins.then_inc(S["dve_chain"], 1)
                dve.wait_ge(S["dve_chain"], chain[0])

            def norm_stats(s, c):
                for t in range(CT):
                    ins = nc.vector.bn_stats(stats[:, t, :], x_tok[:, c * CT + t, :])
                then(ins)
                col = lambda k: stats[:, :, k]
                nc.vector.tensor_tensor(ln_sum[:, c, :], col(1), col(4), ALU.add)
                nc.vector.tensor_tensor(ln_dif[:, c, :], col(1), col(4), ALU.subtract)
                then(nc.vector.tensor_tensor(ln_m2[:, c, :], col(2), col(5), ALU.add))
                nc.vector.tensor_scalar(ln_mean[:, c, :], ln_sum[:, c, :], 0.5, None, ALU.mult)
                then(nc.vector.tensor_tensor(ln_dif[:, c, :], ln_dif[:, c, :], ln_dif[:, c, :], ALU.mult))
                ins = nc.vector.scalar_tensor_tensor(out=ln_m2[:, c, :], in0=ln_dif[:, c, :], scalar=C / 4.0, in1=ln_m2[:, c, :],
                                                     op0=ALU.mult, op1=ALU.add)
                ins.then_inc(S["ln_stats"], 1)

            def norm_scale(s, c):
                l, m = s // 2, (SA, CA) if s % 2 == 0 else (SB, CB)
                dve.wait_ge(S["ln_rstd"], s * NCHUNK + c + 1)
                for t in range(CT):
                    ins = nc.vector.tensor_scalar(h_tok[:, c * CT + t, :], x_tok[:, c * CT + t, :], ln_mean[:, c, t:t + 1],
                                                  ln_rs[:, c, t:t + 1], ALU.subtract, ALU.mult)
                then(ins)
                h = h_tok[:, c * CT:(c + 1) * CT, :]
                wide = lambda k: mod[:, l, c // 2, k, :].unsqueeze(1).broadcast_to([P, CT, C])
                then(nc.vector.tensor_tensor(h, h, wide(m[1]), ALU.mult))
                nc.vector.tensor_tensor(h, h, wide(m[0]), ALU.add).then_inc(S["h_ready"], 1)
                dve.wait_ge(S["h_ready"], s * NCHUNK + c + 1)

            def norm_rows(s, c):
                norm_stats(s, c)
                norm_scale(s, c)

            def take_logits(l, c, e, b):
                dve.wait_ge(S["logit_ps"], l * NCHUNK + c + 1)
                src = ps[:, b, 0:CT * E1].rearrange("p (t e) -> p t e", e=E1)[:, :, 0:e]
                dst = route[:, 0, 0:e * NTILE].rearrange("p (e t) -> p t e", t=NTILE)[:, c * CT:(c + 1) * CT, :]
                if l:
                    ins = nc.vector.tensor_tensor(dst, src, rb1_s[:, :].unsqueeze(1).broadcast_to([P, CT, e]), ALU.add)
                else:
                    ins = nc.vector.tensor_copy(dst, src)
                ins.then_inc(S["logit_sb"], 1)
                dve.wait_ge(S["logit_sb"], l * NCHUNK + c + 1)

            def pick(l, e_n, st):
                n = e_n * NTILE

                def et(r):
                    return route[:, r, 0:n].rearrange("p (e t) -> p e t", t=NTILE)

                def te(r):
                    return route[:, r, 0:n].rearrange("p (e t) -> p t e", t=NTILE)

                def over_e(a):
                    return a.unsqueeze(1).broadcast_to([P, e_n, NTILE])

                iota = cst[:, K["eiota"]][:, 0:e_n].unsqueeze(2).broadcast_to([P, e_n, NTILE])
                for k in range(2):
                    src, best = (0, m12[:, k, :]) if k == 0 else (3, m12[:, k, :])
                    then(nc.vector.tensor_reduce(best, te(src), axis=AX, op=ALU.max))
                    then(nc.vector.tensor_tensor(et(4), et(src), over_e(best), ALU.is_equal))
                    then(nc.vector.tensor_scalar(et(4), et(4), -BIG, BIG, ALU.mult, ALU.add))
                    then(nc.vector.tensor_tensor(et(4), et(4), iota, ALU.add))
                    then(nc.vector.tensor_reduce(low[:, :], te(4), axis=AX, op=ALU.min))
                    then(nc.vector.tensor_tensor(et(1 + k), iota, over_e(low[:, :]), ALU.is_equal))
                    if k == 0:
                        then(nc.vector.scalar_tensor_tensor(out=et(3), in0=et(1), scalar=LOWEST, in1=et(0), op0=ALU.mult, op1=ALU.add))
                nc.vector.tensor_tensor(mask_b[:, 0:n], route[:, 1, 0:n], route[:, 2, 0:n], ALU.add).then_inc(S["mask_ready"], 1)
                if l == 0:
                    nc.vector.tensor_tensor(et(8), et(0), over_e(m12[:, 0, :]), ALU.subtract).then_inc(S["pick_exp"], 1)
                else:
                    nc.vector.tensor_tensor(route[:, 8, 0:NTILE], m12[:, 1, :], m12[:, 0, :], ALU.subtract).then_inc(S["pick_exp"], 1)
                dve.wait_ge(S["rank_ps"], l + 1)
                then(nc.vector.tensor_copy(route[:, 4, 0:n], ps[:, 2, 0:n]))
                then(nc.vector.tensor_tensor_scan(route[:, 5, 0:n], cst[:, K["reset"]][:, 0:n], route[:, 4, 0:n], 0.0, ALU.mult, ALU.add))
                tot = route[:, 5, 0:n].rearrange("p (e t) -> p e t", t=NTILE)[:, :, NTILE - 1]
                then(nc.vector.tensor_scalar(tiles_e[:, 0, 0:e_n], tot, 1.0 / P, 0.5 - 0.5 / P, ALU.mult, ALU.add))
                then(nc.vector.tensor_scalar(tiles_e[:, 1, 0:e_n], tiles_e[:, 0, 0:e_n], MAGIC, MAGIC, ALU.add, ALU.subtract))
                then(nc.vector.tensor_tensor_scan(tiles_e[:, 2, 0:e_n], ones_f[:, 0:e_n], tiles_e[:, 1, 0:e_n], 0.0, ALU.mult, ALU.add))
                then(nc.vector.tensor_tensor(tiles_e[:, 3, 0:e_n], tiles_e[:, 2, 0:e_n], tiles_e[:, 1, 0:e_n], ALU.subtract))
                then(nc.vector.tensor_scalar(tiles_e[:, 3, 0:e_n], tiles_e[:, 3, 0:e_n], float(P), None, ALU.mult))
                then(nc.vector.tensor_tensor(route[:, 5, 0:n], route[:, 5, 0:n], route[:, 4, 0:n], ALU.subtract))
                then(nc.vector.tensor_tensor(route[:, 5, 0:n], route[:, 5, 0:n], ps[:, 1, 0:n], ALU.add))
                then(nc.vector.tensor_tensor(et(5), et(5), tiles_e[:, 3, 0:e_n].unsqueeze(2).broadcast_to([P, e_n, NTILE]), ALU.add))
                for k in range(2):
                    then(nc.vector.tensor_tensor(route[:, 4, 0:n], route[:, 1 + k, 0:n], route[:, 5, 0:n], ALU.mult))
                    then(nc.vector.tensor_reduce(slot_f[:, :], te(4), axis=AX, op=ALU.add))
                    then(nc.vector.tensor_copy(slot_i[:, k, :], slot_f[:, :]))
                cmp = xcmp[0:1, 0:st * e_n].rearrange("p (j e) -> p j e", e=e_n)
                then(nc.vector.tensor_tensor(cmp, cst[0:1, K["jiota"]][:, 0:st].unsqueeze(2).broadcast_to([1, st, e_n]),
                                             tiles_e[0:1, 2, 0:e_n].unsqueeze(1).broadcast_to([1, st, e_n]), ALU.is_ge))
                then(nc.vector.tensor_reduce(tile_f[0:1, 0:st], cmp, axis=AX, op=ALU.add))
                then(nc.vector.tensor_scalar(tile_f[0:1, 0:st], tile_f[0:1, 0:st], float(e_n - 1), None, ALU.min))
                nc.vector.tensor_copy(tile_i[0:1, l, 0:st], tile_f[0:1, 0:st]).then_inc(S["slots_ready"], 1)
                dve.wait_ge(S["slots_ready"], l + 1)
                dve.wait_ge(S["pick_exp_done"], l + 1)
                if l == 0:
                    then(nc.vector.tensor_reduce(ssum[:, :], te(8), axis=AX, op=ALU.add))
                    then(nc.vector.reciprocal(wts[:, 0, :], ssum[:, :]))
                    then(nc.vector.tensor_tensor(et(4), et(8), et(2), ALU.mult))
                    then(nc.vector.tensor_reduce(low[:, :], te(4), axis=AX, op=ALU.add))
                    then(nc.vector.tensor_tensor(wts[:, 1, :], low[:, :], wts[:, 0, :], ALU.mult))
                    then(nc.vector.tensor_tensor(low[:, :], wts[:, 0, :], wts[:, 1, :], ALU.add))
                    then(nc.vector.tensor_scalar(low[:, :], low[:, :], 1e-9, None, ALU.add))
                    then(nc.vector.reciprocal(low[:, :], low[:, :]))
                    then(nc.vector.tensor_tensor(wts[:, 0, :], wts[:, 0, :], low[:, :], ALU.mult))
                    then(nc.vector.tensor_tensor(wts[:, 1, :], wts[:, 1, :], low[:, :], ALU.mult))
                else:
                    ex = route[:, 8, 0:NTILE]
                    then(nc.vector.tensor_scalar(low[:, :], ex, 1.0, None, ALU.add))
                    then(nc.vector.reciprocal(wts[:, 0, :], low[:, :]))
                    then(nc.vector.tensor_tensor(wts[:, 1, :], ex, wts[:, 0, :], ALU.mult))

            dve.wait_ge(S["in_small"], 32)
            nc.vector.tensor_copy(tri_b[:, :], cst[:, K["tri"]]).then_inc(S["dve_chain"], 1)
            chain[0] += 1
            for d in range(ND):
                nc.vector.tensor_scalar(diag_d[:, d, :], ident, d_skip[:, d:d + 1], None, ALU.mult)
            nc.vector.tensor_copy(sel_b[:, :, :], cst[0:3 * 2 * NS, K["sel"]].unsqueeze(2).broadcast_to([3 * 2 * NS, NS, P]))
            dve.wait_ge(S["neg_ready"], 1)
            nc.vector.tensor_scalar(neg_a[:, :, :], neg_a[:, :, :], -1.0, None, ALU.mult).then_inc(S["neg_ready"], 1)
            for c in range(NCHUNK):
                dve.wait_ge(S["in_x"], 16 * NCHUNK)
                norm_stats(0, c)
            for lb, (q0, q1) in enumerate(((1, 2), (3, 4), (5, 6), (7, 0))):
                dve.wait_ge(S["mod_ps"], lb + 1)
                m = mod[:, lb // BATCH, lb % BATCH, :, :].rearrange("p k c -> p (k c)")
                nc.vector.tensor_copy(m[:, 0:CHUNK], bank(q0))
                ins = nc.vector.tensor_copy(m[:, CHUNK:6 * C], ps[:, q1, 0:2 * C])
            ins.then_inc(S["mod_done"], 1)
            dve.wait_ge(S["mod_done"], 1)
            every = mod[:, :, :, :, :].rearrange("p l b k c -> p (l b) k c")
            for k in (CA, CB):
                then(nc.vector.tensor_scalar(every[:, :, k, :], every[:, :, k, :], 1.0, None, ALU.add))
            norm_scale(0, 0)
            dve.wait_ge(S["in_ssm"], 80)
            nc.vector.tensor_tensor(wconv[:, :, :], win_s[:, 0:DIN].unsqueeze(1).broadcast_to([P, TAPS, DIN]), convr_s[:, :, :],
                                    ALU.mult).then_inc(S["w_scaled"], 1)
            norm_scale(0, 1)
            norm_scale(0, 2)
            for k in (GA, GB):
                g = every[:, :, k, :]
                s0 = prod[:, 0, 0, :].rearrange("p (a c) -> p a c", a=4)
                s1 = prod[:, 0, 1, :].rearrange("p (a c) -> p a c", a=4)
                nc.vector.tensor_scalar(s0, g, 0.0, 2.0, ALU.is_ge, ALU.mult)
                then(nc.vector.scalar_tensor_tensor(out=s1, in0=g, scalar=-1.0, in1=g, op0=ALU.mult, op1=ALU.max))
                nc.vector.tensor_scalar(s0, s0, 1.0, None, ALU.subtract)
                then(nc.vector.tensor_scalar(s1, s1, 0.25, None, ALU.max))
                then(nc.vector.tensor_tensor(g, s0, s1, ALU.mult))
            for b in range(BATCH):
                then(nc.vector.tensor_tensor(wout_g[:, b, :, :], wout_s[:, :, :],
                                             mod[:, 0, b, GA, :].unsqueeze(1).broadcast_to([P, ND, C]), ALU.mult))

            def split_rows(c):
                dve.wait_ge(S["bcf_ready"], c + 1)
                q = c % 2
                then(nc.vector.tensor_copy(bc3[0:2 * NS, q, :], bc_f[:, :]))
                then(nc.vector.tensor_tensor(bc_rest[:, :], bc_f[:, :], bc3[0:2 * NS, q, :], ALU.subtract))
                then(nc.vector.tensor_copy(bc_hi[:, :], bc_rest[:, :]))
                nc.vector.tensor_copy(bc3[2 * NS:4 * NS, q, :], bc_hi[:, :])
                nc.vector.tensor_tensor(bc3[4 * NS:6 * NS, q, :], bc_rest[:, :], bc_hi[:, :], ALU.subtract).then_inc(S["bc3_ready"], 1)

            def dt_and_u(c):
                q = c % 2
                for d in range(ND):
                    dve.wait_ge(S["softp_done"], 2 * c + d + 1)
                    then(nc.vector.tensor_tensor(dtT[:, q, d, :], dtT[:, q, d, :], softp[:, d, :], ALU.add))
                    nc.vector.tensor_tensor(uT[:, q, d, :], dtT[:, q, d, :], xcT[:, q, d, :], ALU.mult).then_inc(S["dt_ready"], 1)

            def carries(g):
                return g // (2 * NS) * NS + min(g % (2 * NS), NS)

            def scans(g):
                c, n = divmod(g, NS)
                dve.wait_ge(S["bu_ready"], g + 1)
                if g >= 2:
                    dve.wait_ge(S["prod_ready"], g - 1)
                    dve.wait_ge(S["carried"], carries(g - 1))
                for d in range(ND):
                    dve.wait_ge(S["a_ready"], 2 * g + d + 1)
                    nc.vector.tensor_tensor_scan(hs[:, g % 2, d, :], decay_of(g, d), bu[:, g % 3, d, :],
                                                 carry[:, d, n:n + 1] if c % 2 else 0.0,
                                                 ALU.mult, ALU.add).then_inc(S["scan_done"], 1)

            def products(g):
                c, n = divmod(g, NS)
                dve.wait_ge(S["scan_done"], 2 * g + 2)
                dve.wait_ge(S["c_ps"], g + 1)
                if g >= 3:
                    dve.wait_ge(S["sum_done"], g - 2)
                nc.vector.tensor_tensor(prod[:, g % 3, :, :], hs[:, g % 2, :, :],
                                        bank(C_BANK if g % 2 else TP).unsqueeze(1).broadcast_to([P, ND, CHUNK]),
                                        ALU.mult).then_inc(S["prod_ready"], 1)
                if c % 2 == 0:
                    nc.vector.tensor_copy(carry[:, :, n:n + 1], hs[:, g % 2, :, CHUNK - 1:CHUNK]).then_inc(S["carried"], 1)

            def gate_y(c):
                dve.wait_ge(S["sum_done"], (c + 1) * NS)
                dve.wait_ge(S["zs_ready"], 2 * c + 2)
                if c:
                    dve.wait_ge(S["o_ps"], c)
                nc.vector.tensor_tensor(yT[:, :, :], bank(Y_BANK, 2), zsT[:, c % 2, :, :], ALU.mult).then_inc(S["y_ready"], 1)

            def add_x(c):
                dve.wait_ge(S["o_ps"], c + 1)
                xs = x_tok[:, c * CT:(c + 1) * CT, :]
                nc.vector.tensor_tensor(xs, xs, bank(W0).rearrange("p (t c) -> p t c", c=C), ALU.add).then_inc(S["x_added"], 1)
                dve.wait_ge(S["x_added"], c + 1)
                norm_stats(1, c)

            before = {11: split_rows, 13: dt_and_u}
            after = {1: gate_y, 5: add_x, 7: lambda c: norm_scale(1, c), 15: lambda c: take_logits(0, c, E0, W1)}
            norm_scale(0, 3)
            split_rows(0)
            dt_and_u(0)
            for g in range(STEPS):
                c, n = divmod(g, NS)
                scans(g)
                if g:
                    products(g - 1)
                if n in before and c + 1 < NCHUNK:
                    before[n](c + 1)
                if n in after and c:
                    after[n](c - 1)
            products(STEPS - 1)
            for n in sorted(after):
                after[n](NCHUNK - 1)
            pick(0, E0, ST0)
            dve.wait_ge(S["in_w1"], 16 * (3 * E0 + 1))
            dve.sem_inc(S["up_sb0"], 2)
            dve.sem_inc(S["dn_sb0"], 2)

            def at(j):
                return slice(j, j + 1) if isinstance(j, int) else bass.ds(j, 1)

            def expert_of(l, j, n):
                return dve.value_load(tile_i[0:1, l, at(j)], min_val=0, max_val=n - 1)

            def bias_up(j, u):
                e = expert_of(0, j, E0)
                dve.wait_ge(S["up_ps0"], j + 3)
                nc.vector.tensor_tensor(hp0[:, u, :], bank(2 + u), b1_s[:, bass.ds(e, 1), :].rearrange("p a f -> p (a f)"),
                                        ALU.add).then_inc(S["up_sb0"], 1)

            def bias_down(j, j2, u):
                e = expert_of(0, j, E0)
                dve.wait_ge(S["dn_ps0"], j + 3)
                if j2 is not None:
                    dve.wait_ge(saved[0, u], j2 * 16)
                nc.vector.tensor_tensor(ys0[:, u, :], ps[:, 6 + u, 0:C], b2_s[:, bass.ds(e, 1), :].rearrange("p a c -> p (a c)"),
                                        ALU.add).then_inc(S["dn_sb0"], 1)

            bias_up(0, 0)
            bias_up(1, 1)
            for u in range(2):
                bias_up(u + 2, u)
                bias_down(u, None, u)
            with dve.Fori(0, (ST0 - 4) // 4) as i:
                for k in range(4):
                    bias_up(i * 4 + (k + 4), k % 2)
                    bias_down(i * 4 + (k + 2), i * 2 + (1 + k // 2), k % 2)
            for u in range(2):
                bias_down(ST0 - 2 + u, ST0 // 2 - 1, u)
            def weigh(c, l, y, o):
                dve.wait_ge(gathered[l, c], 16 * 2 * CT)
                for t in range(c * CT, (c + 1) * CT):
                    ins = nc.vector.tensor_scalar(y[0][:, t, :], y[0][:, t, :], wts[:, 0, t:t + 1], None, ALU.mult)
                then(ins)
                for t in range(c * CT, (c + 1) * CT):
                    ins = nc.vector.scalar_tensor_tensor(out=o[:, t, :], in0=y[1][:, t, :], scalar=wts[:, 1, t:t + 1],
                                                         in1=y[0][:, t, :], op0=ALU.mult, op1=ALU.add)
                return ins

            def experts_in(c):
                ts = slice(c * CT, (c + 1) * CT)
                then(weigh(c, 0, y0, y0[0]))
                then(nc.vector.tensor_tensor(y0[0][:, ts, :], y0[0][:, ts, :], mod[:, 0, c // 2, GB, :].unsqueeze(1).broadcast_to([P, CT, C]), ALU.mult))
                then(nc.vector.tensor_tensor(x_tok[:, ts, :], x_tok[:, ts, :], y0[0][:, ts, :], ALU.add))
                norm_stats(2, c)

            def rms_scale(c):
                dve.wait_ge(S["rms_sum"], c + 1)
                for t in range(c * CT, (c + 1) * CT):
                    ins = nc.vector.tensor_scalar(xn_tok[:, t, :], h_tok[:, t, :], rms_ss[:, t:t + 1], None, ALU.mult)
                ins.then_inc(S["xn_ready"], 1)

            def gated_scan(c):
                cs = slice(c * CHUNK, (c + 1) * CHUNK)
                dve.wait_ge(S["p4_side"], c + 1)
                nc.vector.tensor_tensor(bT[:, cs], bank(PROJ[c % 2][1]), sideT[:, cs], ALU.mult).then_inc(S["b_gated"], 1)
                dve.wait_ge(S["b_gated"], c + 1)
                dve.wait_ge(S["p4_a"], c + 1)
                then(nc.vector.tensor_tensor_scan(scanT[:, cs], aT[:, cs], bT[:, cs], scanT[:, c * CHUNK - 1:c * CHUNK] if c % 2 else 0.0,
                                                  ALU.mult, ALU.add))
                dve.wait_ge(S["p4_gate"], c + 1)
                nc.vector.tensor_tensor(gateT[:, cs], gateT[:, cs], scanT[:, cs], ALU.mult).then_inc(S["gated_y"], 1)

            def attention_in(c):
                ts = slice(c * CT, (c + 1) * CT)
                dve.wait_ge(S["o_ps"], NCHUNK + c + 1)
                dve.wait_ge(S["res_ready"], c + 1)
                then(nc.vector.tensor_tensor(x_tok[:, ts, :], x_tok[:, ts, :], bank(PROJ[c % 2][1]).rearrange("p (t c) -> p t c", c=C), ALU.add))
                nc.vector.tensor_tensor(x_tok[:, ts, :], x_tok[:, ts, :], h_tok[:, ts, :], ALU.add).then_inc(S["x_added"], 1)
                dve.wait_ge(S["x_added"], NCHUNK + c + 1)
                norm_stats(3, c)

            for c in range(NCHUNK + 2):
                if c < NCHUNK:
                    experts_in(c)
                if 0 < c <= NCHUNK:
                    norm_scale(2, c - 1)
                if c == 1:
                    dve.wait_ge(S["in_l1"], 32)
                    then(nc.vector.tensor_scalar(w4_s[:, :, :], w4_s[:, :, :], vec[:, V["rmsw"]], None, ALU.mult))
                    nc.vector.tensor_tensor(wo_g[:, :, :], mod[:, 1, :, GA, :], wo_s[:, :].unsqueeze(1).broadcast_to([P, BATCH, C]),
                                            ALU.mult).then_inc(S["w_scaled"], 1)
                if c > 1:
                    rms_scale(c - 2)
            gated_scan(0)
            gated_scan(1)
            attention_in(0)
            gated_scan(2)
            attention_in(1)
            gated_scan(3)
            dve.wait_ge(S["in_nw"], 32)
            norm_scale(3, 0)
            attention_in(2)
            norm_scale(3, 1)
            attention_in(3)
            norm_scale(3, 2)
            take_logits(1, 0, E1, PROJ[0][1])
            norm_scale(3, 3)
            for c in range(1, NCHUNK):
                take_logits(1, c, E1, PROJ[c % 2][1])
            pick(1, E1, ST1)
            dve.wait_ge(S["phase_done"], 2)
            dve.sem_inc(S["up_sb1"], GT)

            def take_up(j, u):
                e = expert_of(1, j, E1)
                js = bass.ds(j, 1)
                dve.wait_ge(S["up_abs1"], j + 1)
                nc.vector.tensor_copy(mag[:, js, :].rearrange("p a h -> p (a h)"), ps[:, 2 + u, 0:H1])
                nc.vector.scalar_tensor_tensor(out=freq[:, js, :].rearrange("p a h -> p (a h)"), in0=ps[:, 2 + u, H1:2 * H1], scalar=0.0,
                                               in1=phase_s[:, bass.ds(e, 1), :].rearrange("p a h -> p (a h)"),
                                               op0=ALU.max, op1=ALU.add).then_inc(S["up_sb1"], 1)

            def argument(g, q):
                gs = bass.ds(g * GT, GT)
                dve.wait_ge(S["soft_l1"], g + 1)
                dve.wait_ge(S["up_sb1"], g * GT + 2 * GT)
                nc.vector.scalar_tensor_tensor(out=freq[:, gs, :], in0=fabs[:, q, :, :], scalar=1.0 / (2 * PI), in1=freq[:, gs, :],
                                               op0=ALU.mult, op1=ALU.add).then_inc(S["theta1"], 1)

            def turn(g, q):
                gs = bass.ds(g * GT, GT)
                dve.wait_ge(S["theta1"], g + 3)
                dve.wait_ge(S["turned1"], g + 1)
                nc.vector.tensor_scalar(hold[:, q, :, :], freq[:, gs, :], MAGIC, MAGIC, ALU.add, ALU.subtract).then_inc(S["whole1"], 1)

            def take_group(g, g1=None, q=0):
                for k in range(GT):
                    take_up(g * GT + k, k)
                    if g1 is not None and k == 1:
                        argument(g1, q)
                    if g1 is not None and k == 2:
                        turn(g1, q)

            dve.sem_inc(S["turned1"], 2)
            take_group(0)
            with dve.Fori(0, NG // 2 - 1) as i:
                for q in range(2):
                    take_group(i * 2 + (q + 1), i * 2 + q, q)
            take_group(NG - 1, NG - 2, 0)
            argument(NG - 1, 1)
            turn(NG - 1, 1)
            dve.sem_inc(S["ht_sb1"], 2)
            dve.sem_inc(S["dn_sb1"], 2)

            def hidden(j, g, u):
                js = bass.ds(j, 1)
                dve.wait_ge(S["cos1"], g + 1)
                nc.vector.tensor_tensor(hd1[:, u, :], mag[:, js, :].rearrange("p a h -> p (a h)"), freq[:, js, :].rearrange("p a h -> p (a h)"),
                                        ALU.mult).then_inc(S["hid1"], 1)

            def copy_ht(j, u):
                dve.wait_ge(S["ht_ps1"], j + 3)
                nc.vector.tensor_copy(ht1[:, u, :], ps[:, 4 + u, 0:H1]).then_inc(S["ht_sb1"], 1)

            def copy_y(j, g, k):
                dve.wait_ge(S["dn_ps1"], j + 3)
                if g is not None:
                    dve.wait_ge(saved[1, k], g * 16)
                nc.vector.tensor_copy(ys1[:, k, :], ps[:, 6 + k % 2, 0:C]).then_inc(S["dn_sb1"], 1)

            hidden(0, 0, 0)
            hidden(1, 0, 1)
            copy_ht(0, 0)

            def down_steps(j0, g, stored):
                for k in range(GT):
                    hidden(j0 + (k + 2), g + (k + 2) // GT, k % 2)
                    copy_ht(j0 + (k + 1), (k + 1) % 2)
                    copy_y(j0 + k, stored, k)

            down_steps(0, 0, None)
            with dve.Fori(0, ST1 // GT - 2) as i:
                down_steps(i * GT + GT, i + 1, i + 1)
            for j in range(ST1 - GT, ST1):
                if j + 2 < ST1:
                    hidden(j + 2, (j + 2) // GT, j % 2)
                if j + 1 < ST1:
                    copy_ht(j + 1, (j + 1) % 2)
                copy_y(j, j // GT, j % GT)
            nc.vector.tensor_tensor(mod[:, 1, :, GB, :], mod[:, 1, :, GB, :], nw_s[:, :].unsqueeze(1).broadcast_to([P, BATCH, C]),
                                    ALU.mult).then_inc(S["dve_chain"], 1)
            chain[0] += 1
            for c in range(NCHUNK + 1):
                if c < NCHUNK:
                    weigh(c, 1, y1, o1).then_inc(S["o_mix"], 1)
                if c == 0:
                    continue
                dve.wait_ge(S["o_rstd"], c)
                dve.wait_ge(S["dve_chain"], chain[0])
                dve.wait_ge(S["o_mix"], c)
                ts = slice((c - 1) * CT, c * CT)
                for t in range((c - 1) * CT, c * CT):
                    ins = nc.vector.tensor_scalar(o1[:, t, :], o1[:, t, :], ssum[:, t:t + 1], None, ALU.mult)
                then(ins)
                then(nc.vector.tensor_tensor(o1[:, ts, :], o1[:, ts, :], mod[:, 1, (c - 1) // 2, GB, :].unsqueeze(1).broadcast_to([P, CT, C]), ALU.mult))
                nc.vector.tensor_tensor(x_tok[:, ts, :], x_tok[:, ts, :], o1[:, ts, :], ALU.add).then_inc(S["o_final"], 1)


def kernel(**inputs):
    import numpy as np
    import concourse.bacc as bacc
    from concourse import mybir as _mybir
    from concourse.bass_utils import run_bass_kernel_spmd as run

    w = {k: np.asarray(v) for k, v in inputs.items()}

    def halves(a):
        return a.reshape(ND, P, -1).transpose(1, 0, 2)

    def flat(a):
        return a.reshape(a.shape[0], -1)

    vecs = np.concatenate([
        flat(halves(w["L0_attn_conv_w"])), flat(halves(w["L0_attn_conv_b"])), flat(halves(w["L0_attn_b_dt"])),
        flat(halves(w["L0_attn_A_log"])), flat(halves(w["L0_attn_D_param"])), w["L0_c"].T, w["L1_c"].T,
        w["L1_attn_rms_weight"][:, None], w["L1_attn_b_A"][:, None], w["L0_ffn_router_w"].T, w["L1_ffn_router_w"].T], axis=1)
    consts = np.zeros((P, NCONST), np.float32)
    part, col = np.arange(P)[:, None], np.arange(P)[None, :]
    consts[:, K["ident"]] = part == col
    consts[:, K["tri"]] = part < col
    consts[:, K["sel"]] = part % (2 * NS) == NS + np.arange(NS)[None, :]
    consts[:, K["eiota"]] = np.arange(E1)
    consts[:, K["jiota"]] = np.arange(ST1)
    consts[:, K["reset"]] = np.arange(E1 * NTILE) % NTILE != 0
    arrays = {
        "x": w["L0_attn_x"].reshape(T, C),
        "consts": consts,
        "vecs": vecs,
        "w_in": w["L0_attn_W_in"].T,
        "conv_rows": w["L0_attn_conv_w"].T,
        "w_x": halves(w["L0_attn_W_x"].T),
        "w_dt": w["L0_attn_W_dt"].T,
        "w_out": halves(w["L0_attn_W_out"].T),
        "w1": w["L0_ffn_w1"].transpose(2, 0, 1),
        "b1": w["L0_ffn_b1"],
        "w2": w["L0_ffn_w2"].reshape(E0, C, FK0, P).transpose(3, 0, 2, 1),
        "b2": w["L0_ffn_b2"],
        "wmod": np.stack([w["L0_wmod"], w["L1_wmod"]], axis=1),
        "w4": np.stack([w["L1_attn_w_A"], w["L1_attn_w_x"], w["L1_attn_w_output"], w["L1_attn_w_sidegate"]], axis=1),
        "wo": w["L1_attn_w_o"],
        "mf": np.concatenate([w["L1_ffn_bank_mag"], w["L1_ffn_bank_freq"]], axis=2).transpose(1, 0, 2),
        "phase": w["L1_ffn_bank_phase"],
        "down": w["L1_ffn_bank_down"].reshape(E1, FK1, P, C).transpose(2, 0, 1, 3),
        "norm_w": w["L1_ffn_norm_w"],
        "rbias1": w["L1_ffn_router_bias"],
    }
    nc = bacc.Bacc("TRN2", target_bir_lowering=False, num_devices=1)
    ins, aps = {}, []
    for name, a in arrays.items():
        a = np.ascontiguousarray(a)
        ins[f"in_{name}"] = a
        aps.append(nc.dram_tensor(f"in_{name}", a.shape, _mybir.dt.from_np(a.dtype), kind="ExternalInput").ap())
    out = nc.dram_tensor("out_0", (T, C), F32, kind="ExternalOutput").ap()
    adaln_two_layers(nc, *aps, out)
    r = run(nc, [ins], core_ids=[0])
    return r.results[0]["out_0"].reshape(BATCH, SEQ, C)
```
